# Optimizing a Trainium2 kernel written in Bass

```python
import numpy as np
import jax
import jax.numpy as jnp

def _softmax(x, axis=-1):
    return jax.nn.softmax(x, axis=axis)

def _gelu(x):
    return jax.nn.gelu(x, approximate=True)

def _silu(x):
    return jax.nn.silu(x)

def _sigmoid(x):
    return jax.nn.sigmoid(x)

def _layernorm(x, axis=-1, eps=1e-05):
    m = jnp.mean(x, axis=axis, keepdims=True)
    v = jnp.var(x, axis=axis, keepdims=True)
    return (x - m) / jnp.sqrt(v + eps)

def _scatter_add(tgt, idx, src, axis=0):
    return tgt.at[idx].add(src)

def _segment_sum(src, seg, n):
    return jax.ops.segment_sum(src, seg, n)
kernel_name = 'mk_adj_resnorm_d1_adj_r2_447996'

def setup_inputs(seed: int=0):
    np.random.seed(seed)
    _w = jnp.asarray

    def _rec_inputs():
        import jax
        import jax.numpy as jnp
        _gk = jax.random.key(seed)
        x = -0.0001538 + 1 * jax.random.normal(jax.random.fold_in(_gk, 1), (32, 256, 384), jnp.float32)
        _a = jax.random.bernoulli(jax.random.fold_in(_gk, 2), 0.03125, (32, 256, 256))
        _a = jnp.logical_or(_a, jnp.swapaxes(_a, -1, -2))
        _a = jnp.logical_or(_a, jnp.eye(256, dtype=bool))
        _af = _a.astype(jnp.float32)
        _af = _af * jax.random.uniform(jax.random.fold_in(_gk, 3), (32, 256, 256), jnp.float32, 0.05, 4.42607)
        adj = _af
        return (x, adj)
    x, adj = _rec_inputs()

    def _L0_gnn_setup():
        import jax, jax.numpy as jnp
        import numpy as np
        NUM_HEADS = 12
        HIDDEN = 384
        HEAD = HIDDEN // NUM_HEADS
        SCALE = HIDDEN ** (-0.5)
        key = jax.random.key(seed)
        ks = jax.random.split(key, 8)
        B, N = (16, 256)
        std = HIDDEN ** (-0.5)
        return {'x': jax.random.normal(ks[0], (B, N, HIDDEN), dtype=jnp.float32), 'encoding_bias': jax.random.normal(ks[1], (B, N, N), dtype=jnp.float32), 'Wq': jax.random.normal(ks[2], (HIDDEN, HIDDEN), dtype=jnp.float32) * std, 'Wk': jax.random.normal(ks[3], (HIDDEN, HIDDEN), dtype=jnp.float32) * std, 'Wv': jax.random.normal(ks[4], (HIDDEN, HIDDEN), dtype=jnp.float32) * std, 'bv': jax.random.normal(ks[5], (HIDDEN,), dtype=jnp.float32) * 0.01, 'Wo': jax.random.normal(ks[6], (HIDDEN, HIDDEN), dtype=jnp.float32) * std, 'bo': jax.random.normal(ks[7], (HIDDEN,), dtype=jnp.float32) * 0.01}
    _L0_gnn_all = _L0_gnn_setup()
    _L0_gnn_in = {k: v for k, v in _L0_gnn_all.items() if k in ('Wq', 'Wk', 'Wv', 'bv', 'Wo', 'bo')}
    del _L0_gnn_all
    return {'x': x, 'adj': adj, 'L0_gnn_Wq': _L0_gnn_in['Wq'], 'L0_gnn_Wk': _L0_gnn_in['Wk'], 'L0_gnn_Wv': _L0_gnn_in['Wv'], 'L0_gnn_bv': _L0_gnn_in['bv'], 'L0_gnn_Wo': _L0_gnn_in['Wo'], 'L0_gnn_bo': _L0_gnn_in['bo']}

def reference(x, adj, L0_gnn_Wq, L0_gnn_Wk, L0_gnn_Wv, L0_gnn_bv, L0_gnn_Wo, L0_gnn_bo):
    import jax
    import jax.numpy as jnp

    def _L0_gnn_ref(x, encoding_bias, Wq, Wk, Wv, bv, Wo, bo):
        import jax, jax.numpy as jnp
        import numpy as np
        NUM_HEADS = 12
        HIDDEN = 384
        HEAD = HIDDEN // NUM_HEADS
        SCALE = HIDDEN ** (-0.5)
        B, N, _ = x.shape
        q = (x @ Wq.T).reshape(B, N, NUM_HEADS, HEAD)
        k = (x @ Wk.T).reshape(B, N, NUM_HEADS, HEAD)
        v = (x @ Wv.T + bv).reshape(B, N, NUM_HEADS, HEAD)
        a = jnp.einsum('bnhd,bmhd->bhnm', q, k) * SCALE + encoding_bias[:, None, :, :]
        pad_mask = jnp.all(a == 0, axis=-1)
        a = jnp.where(pad_mask[..., None], -jnp.inf, a)
        a = jax.nn.softmax(a, axis=-1)
        a = jnp.nan_to_num(a)
        o = jnp.einsum('bhnm,bmhd->bnhd', a, v).reshape(B, N, HIDDEN)
        return o @ Wo.T + bo
    x = _layernorm(x + _L0_gnn_ref(x, adj, L0_gnn_Wq, L0_gnn_Wk, L0_gnn_Wv, L0_gnn_bv, L0_gnn_Wo, L0_gnn_bo), axis=-1)
    return x

_drawn_inputs = setup_inputs


def setup_inputs(seed=0):
    import zlib

    import numpy as np

    out = dict(_drawn_inputs(seed))
    spreads = {}
    factors = {'L0_gnn_bv': 5.199, 'L0_gnn_bo': 5.737}
    for name, (base, spread) in spreads.items():
        noise = np.random.default_rng([zlib.crc32(name.encode()), seed]).standard_normal(out[name].shape)
        drawn = base * np.exp(spread * noise) if base else spread * noise
        out[name] = jnp.asarray(drawn.astype(out[name].dtype))
    for name, factor in factors.items():
        out[name] = (out[name] * factor).astype(out[name].dtype)
    return out
```

```python
import concourse.bass as bass
from concourse import mybir

F32 = mybir.dt.float32
F32R = mybir.dt.float32r
I32 = mybir.dt.int32
ALU = mybir.AluOpType
ACT = mybir.ActivationFunctionType
AX = mybir.AxisListType

B, N, D = 32, 256, 384
H, HD = 12, 32
P = 128
KC = D // P
NT = N // P
JH = P // HD
SCALE = D ** -0.5
EPS = 1e-5
BIG = 3.0e38

S_BANKS, P_RING, PT_RING = 3, 4, 6
DMA = 16
STACK_DMAS = 6
DVE_STEPS = 5


class Step:

    def __init__(self, i, c):
        self.i, self.c, self.n, self.p = i, c, 2 * i + c, c % 2
        looped = not isinstance(i, int)
        self.attend = looped or 0 <= c < B
        self.finish = looped or c >= 1
        self.project = looped or c <= B - 2
        self.looped = looped

    def count(self, per_step, extra=0):
        return self.i * (2 * per_step) + (self.c * per_step + extra)

    def units(self):
        order = []
        if self.finish:
            order += ["flag"]
        if self.project:
            order += ["K01"]
        if self.finish:
            order += ["sumT"]
        if self.project:
            order += ["K2Q0"]
        if self.finish:
            order += ["R01", "R2"]
        if self.project:
            order += ["Q12", "V0", "V1"]
        if self.finish:
            order += ["Y0", "Y1"]
        return order

    def units_before(self, name=None):
        k = 0 if name is None else self.units().index(name)
        if self.c == -1 and not self.looped:
            return k
        if self.c == 0 and not self.looped:
            return 5 + k
        if self.c == B and not self.looped:
            return 11 * (B - 1) - 1 + 6 + k
        return self.count(11, k - 1)

    def bank(self, name):
        k = 0 if name is None else self.units().index(name)
        if self.looped or 1 <= self.c < B:
            return (11 * self.c + k - 1) % 2
        return self.units_before(name) % 2

    def head(self, h):
        return (self, h) if h >= 0 else (Step(self.i, self.c - 1), h + H)


def on_dve(h):
    return h % 3 == 1


def dve_heads(t, h):
    return t.count(H // 3, (h + 2) // 3)


def act_heads(t, h):
    return t.count(H - H // 3, h + 1 - (h + 2) // 3)


def steps(eng, body):
    for c in range(-1, 3):
        body(Step(0, c))
    with eng.Fori(1, (B - 4) // 2) as i:
        body(Step(i, 1))
        body(Step(i, 2))
    for c in range(B - 3, B + 1):
        body(Step(0, c))


def build(nc, x, xT, adj, wqT, wkT, wvT, bv, woT, bo, out):
    def sb(name, shape, dt=F32):
        return nc.alloc_sbuf_tensor(name, shape, dt)

    ident = sb("ident", [P, P])
    ones = sb("ones", [P, 1])
    sel_f = sb("sel_f", [H, D])
    sel = sb("sel", [H, D], F32R)
    halfs = sb("halfs", [P, NT])
    w_hi = sb("w_hi", [P, 4, KC, D], F32R)
    w_lo = sb("w_lo", [P, 4, KC, D], F32R)
    bv_all = sb("bv_all", [P, D])
    bo_all = sb("bo_all", [P, D])
    xt = [sb(f"xt{p}", [P, KC, N]) for p in range(2)]
    xt_hi = [sb(f"xt_hi{p}", [P, KC, N], F32R) for p in range(2)]
    xt_lo = [sb(f"xt_lo{p}", [P, KC, N], F32R) for p in range(2)]
    xr = [sb(f"xr{p}", [P, NT, D]) for p in range(2)]
    bias = [sb(f"bias{p}", [P, NT, N]) for p in range(2)]
    kq_hi = sb("kq_hi", [P, 2 * KC, N], F32R)
    kq_lo = sb("kq_lo", [P, 2 * KC, N], F32R)
    k_stack = [sb(f"k_stack{p}", [3 * HD, H, N], F32R) for p in range(2)]
    q_stack = [sb(f"q_stack{p}", [3 * HD, H, N], F32R) for p in range(2)]
    v = [sb(f"v{p}", [P, NT, D]) for p in range(2)]
    neg = sb("neg", [P, H, NT, N])
    w_f = (neg[:, 0:4 * KC * D // (NT * N)].rearrange("p h c n -> p (h c n)")
           .rearrange("p (w k d) -> p w k d", w=4, k=KC))
    negmax = [sb(f"negmax{p}", [P, NT, H]) for p in range(2)]
    sums = [sb(f"sums{p}", [P, NT, H]) for p in range(2)]
    prob = sb("prob", [P, P_RING, NT, N])
    probT = sb("probT", [P, PT_RING, NT, N])
    zero_max = sb("zero_max", [P, NT, H])
    zero_rows = sb("zero_rows", [P, 1])
    zero_flag = sb("zero_flag", [1, 1], I32)
    most = sb("most", [P, NT, H])
    keep = sb("keep", [P, NT, H])
    recip = sb("recip", [P, NT, H])
    inv = sb("inv", [P, NT, H])
    inv_hi = sb("inv_hi", [H, N], F32R)
    inv_lo = sb("inv_lo", [H, N], F32R)
    o_raw = [sb(f"o_raw{p}", [P, KC, N]) for p in range(2)]
    o_n = sb("o_n", [P, KC, N])
    o_hi = sb("o_hi", [P, KC, N], F32R)
    o_lo = sb("o_lo", [P, KC, N], F32R)
    y = sb("y", [P, NT, D])
    stats = sb("stats", [P, NT, 6])
    meanvar = sb("meanvar", [P, NT, 2])
    var_eps = sb("var_eps", [P, NT])
    rstd = sb("rstd", [P, NT])
    y_out = sb("y_out", [P, NT, D])

    s_bank = [nc.alloc_psum_tensor(f"s_bank{k}", [P, NT, N], F32) for k in range(S_BANKS)]
    t_bank = [nc.alloc_psum_tensor(f"t_bank{k}", [P, NT, N], F32) for k in range(2)]
    o_bank = nc.alloc_psum_tensor("o_bank", [P, NT * N], F32)
    shared = [nc.alloc_psum_tensor(f"shared{k}", [P, NT * N], F32) for k in range(2)]

    sem = nc.alloc_semaphore
    const_ready = sem("const_ready")
    w_loaded = sem("w_loaded")
    b_loaded = sem("b_loaded")
    w_scaled = sem("w_scaled")
    w_hi_ready = sem("w_hi_ready")
    w_ready = sem("w_ready")
    xt_loaded = [sem(f"xt_loaded{p}") for p in range(2)]
    xr_loaded = [sem(f"xr_loaded{p}") for p in range(2)]
    bias_loaded = [sem(f"bias_loaded{p}") for p in range(2)]
    xt_hi_ready = sem("xt_hi_ready")
    xt_ready = sem("xt_ready")
    xr_ready = sem("xr_ready")
    kq_hi_ready = sem("kq_hi_ready")
    stacked = [sem(f"stacked{j}") for j in range(JH)]
    scored = sem("scored")
    neg_ready = sem("neg_ready")
    prob_ready = sem("prob_ready")
    transposed = sem("transposed")
    probT_dve = sem("probT_dve")
    probT_act = sem("probT_act")
    pv_done = sem("pv_done")
    o_saved = sem("o_saved")
    unit_done = sem("unit_done")
    unit_free = sem("unit_free")
    zero_counted = sem("zero_counted")
    dve_step = sem("dve_step")
    inv_ready = sem("inv_ready")
    o_hi_ready = sem("o_hi_ready")
    o_ready = sem("o_ready")
    stats_ready = sem("stats_ready")
    var_ready = sem("var_ready")
    rstd_ready = sem("rstd_ready")
    y_ready = sem("y_ready")
    stored = sem("stored")
    passed = sem("passed")

    W_Q, W_K, W_V, W_O = range(4)
    KQ = {"K01": [(W_K, 0), (W_K, 1)], "K2Q0": [(W_K, 2), (W_Q, 0)], "Q12": [(W_Q, 1), (W_Q, 2)]}
    KQ_AT = {"K01": 0, "K2Q0": 2, "Q12": 4}

    def apart(eng):
        eng.sem_inc(passed, 1)

    with nc.Block() as block:

        @block.sync
        def _(sp):
            def load_xt(t, k):
                sp.dma_start(xt[(t.c + k) % 2][:], xT[t.n + k].rearrange("(c p) n -> p c n", p=P)
                             ).then_inc(xt_loaded[(t.c + k) % 2], DMA)

            load_xt(Step(0, 0), 0)
            for w, src in ((W_K, wkT), (W_Q, wqT), (W_V, wvT), (W_O, woT)):
                sp.dma_start(w_f[:, w], src.rearrange("(c p) n -> p c n", p=P)).then_inc(w_loaded, DMA)
            load_xt(Step(0, 0), 1)
            for dst, src in ((bv_all, bv), (bo_all, bo)):
                sp.dma_start(dst[:], src.rearrange("(a n) -> a n", a=1).to_broadcast([P, D])
                             ).then_inc(b_loaded, DMA)

            def stack(t, k, group):
                dst = (k_stack, q_stack)[k][(t.c + 1) % 2]
                for r, part in enumerate(((kq_hi, kq_hi, kq_lo), (kq_hi, kq_lo, kq_hi))[k]):
                    sp.dma_start(dst[HD * r:HD * (r + 1), KC * group:KC * (group + 1), :].bitcast(F32),
                                 part[HD * group:HD * (group + 1), KC * k:KC * (k + 1), :].bitcast(F32)
                                 ).then_inc(stacked[group], DMA)

            def step(t):
                if t.looped or t.c <= B - 4:
                    sp.wait_ge(xt_ready, t.count(1, 2))
                    load_xt(t, 3)
                if t.project:
                    q = (t.c + 1) % 2
                    if t.looped or t.c >= 1:
                        sp.wait_ge(neg_ready, t.count(H * NT))
                    sp.dma_start(bias[q][:], adj[t.n + 1].rearrange("(c p) m -> p c m", p=P)
                                 ).then_inc(bias_loaded[q], DMA)
                if t.attend:
                    if t.looped or t.c >= 2:
                        sp.wait_ge(unit_free, t.units_before())
                    sp.dma_start(xr[t.p][:], x[t.n].rearrange("(c p) d -> p c d", p=P)
                                 ).then_inc(xr_loaded[t.p], DMA)
                if t.project:
                    if t.looped or t.c >= 1:
                        sp.wait_ge(scored, t.count(H))
                        apart(sp)
                    sp.wait_ge(kq_hi_ready, t.count(3, 3 + 2))
                    apart(sp)
                    sp.wait_ge(unit_free, t.units_before("K2Q0") + 1)
                    for group in range(JH):
                        stack(t, 0, group)
                    sp.wait_ge(kq_hi_ready, t.count(3, 3 + 3))
                    apart(sp)
                    sp.wait_ge(unit_free, t.units_before("Q12") + 1)
                    for group in range(JH):
                        stack(t, 1, group)
                if t.finish:
                    sp.wait_ge(y_ready, t.count(NT))
                    sp.dma_start(out[t.n - 1].rearrange("(c p) d -> p c d", p=P), y_out[:]
                                 ).then_inc(stored, DMA)

            steps(sp, step)
            sp.wait_ge(stored, DMA * B)

        @block.gpsimd
        def _(pool):
            nc.gpsimd.memset(ident[:], 0.0).then_inc(const_ready, 1)
            nc.gpsimd.memset(sel_f[:], 1.0).then_inc(const_ready, 1)
            nc.gpsimd.memset(ones[:], 1.0).then_inc(const_ready, 1)
            nc.gpsimd.memset(halfs[:], -0.5).then_inc(const_ready, 1)
            pool.wait_ge(const_ready, 4)
            nc.gpsimd.affine_select(out=ident[:], in_=ident[:], compare_op=ALU.not_equal, fill=1.0,
                                    base=0, pattern=[[-1, P]], channel_multiplier=1).then_inc(const_ready, 1)
            nc.gpsimd.affine_select(out=sel_f[:], in_=sel_f[:], compare_op=ALU.is_ge, fill=0.0,
                                    base=0, pattern=[[1, D]], channel_multiplier=-HD).then_inc(const_ready, 1)
            pool.wait_ge(const_ready, 6)
            nc.gpsimd.affine_select(out=sel_f[:], in_=sel_f[:], compare_op=ALU.is_ge, fill=0.0,
                                    base=HD - 1, pattern=[[-1, D]], channel_multiplier=HD).then_inc(const_ready, 1)
            pool.wait_ge(const_ready, 7)
            nc.gpsimd.tensor_copy(sel[:], sel_f[:]).then_inc(const_ready, 1)

            def split_xt(t, k):
                q = (t.c + k) % 2
                pool.wait_ge(xt_loaded[q], DMA * ((t.c + k) // 2 + 1) + t.i * DMA)
                apart(pool)
                nc.gpsimd.tensor_copy(xt_hi[q][:], xt[q][:]).then_inc(xt_hi_ready, 1)
                pool.wait_ge(xt_hi_ready, t.count(1, k + 1))
                nc.gpsimd.tensor_tensor(xt_lo[q][:], xt[q][:], xt_hi[q][:].bitcast(F32), ALU.subtract
                                        ).then_inc(xt_ready, 1)

            split_xt(Step(0, 0), 0)

            def step(t):
                if t.looped or t.c <= B - 3:
                    if t.looped or t.c >= 0:
                        pool.wait_ge(unit_done, t.units_before())
                    split_xt(t, 2)
                if t.attend:
                    pool.wait_ge(b_loaded, 2 * DMA)
                    pool.wait_ge(xr_loaded[t.p], DMA * (t.c // 2 + 1) + t.i * DMA)
                    nc.gpsimd.tensor_tensor(xr[t.p][:], xr[t.p][:], bo_all[:].unsqueeze(1).to_broadcast([P, NT, D]),
                                            ALU.add).then_inc(xr_ready, 1)
                if t.finish:
                    pool.wait_ge(unit_free, t.units_before("R2") + 1)
                    if t.looped or t.c >= 2:
                        pool.wait_ge(unit_done, t.units_before())
                    apart(pool)
                    nc.gpsimd.tensor_copy(o_hi[:], o_n[:]).then_inc(o_hi_ready, 1)
                    pool.wait_ge(o_hi_ready, t.count(1))
                    nc.gpsimd.tensor_tensor(o_lo[:], o_n[:], o_hi[:].bitcast(F32), ALU.subtract
                                            ).then_inc(o_ready, 1)
                    pool.wait_ge(stats_ready, t.count(NT))
                    apart(pool)
                    nc.gpsimd.tensor_scalar(var_eps[:], meanvar[:, :, 1], EPS, None, ALU.add
                                            ).then_inc(var_ready, 1)
                    pool.wait_ge(var_ready, t.count(1))
                    nc.gpsimd.tensor_tensor(rstd[:], var_eps[:], halfs[:], ALU.pow).then_inc(rstd_ready, 1)

            steps(pool, step)

        @block.scalar
        def _(act):
            for k, w in enumerate((W_K, W_Q, W_V, W_O)):
                act.wait_ge(w_loaded, 4 * DMA)
                if w == W_Q:
                    act.wait_ge(w_scaled, 1)
                nc.scalar.activation(w_hi[:, w], w_f[:, w], ACT.Copy).then_inc(w_hi_ready, 1)

            def kq_hi_part(t, name):
                act.wait_ge(unit_done, t.units_before(name) + 1)
                if name == "K01" and (t.looped or t.c >= 0):
                    for group in range(JH):
                        act.wait_ge(stacked[group], t.count(STACK_DMAS * DMA, STACK_DMAS * DMA))
                a = KQ_AT[name]
                nc.scalar.activation(kq_hi[:, a:a + 2, :], shared[t.bank(name)][:].rearrange("p (a n) -> p a n", a=2),
                                     ACT.Copy).then_inc(kq_hi_ready, 1)

            def copy_probT(t, h):
                g = t.count(H, h)
                act.wait_ge(transposed, g + 1)
                if t.looped or g >= PT_RING:
                    act.wait_ge(pv_done, t.count(KC, (h - PT_RING) // JH + 1))
                nc.scalar.activation(probT[:, h % PT_RING], t_bank[h % 2][:], ACT.Copy).then_inc(probT_act, 1)

            def exps(t, h):
                g = t.count(H, h)
                if t.looped or g >= P_RING:
                    act.wait_ge(transposed, g - P_RING + 1)
                for c in range(NT):
                    act.wait_ge(neg_ready, t.count(H * NT, NT * h + c + 1))
                    if h == 0 and (t.looped or t.c >= 2):
                        act.wait_ge(inv_ready, t.count(1, -1))
                    nc.scalar.activation(prob[:, h % P_RING, c], neg[:, h, c], ACT.Exp, scale=-1.0,
                                         bias=negmax[t.p][:, c, h:h + 1], accum_out=sums[t.p][:, c, h:h + 1]
                                         ).then_inc(prob_ready, 1)

            def save_o(t, c):
                act.wait_ge(pv_done, t.count(KC, c + 1))
                if c == 0 and (t.looped or t.c >= 2):
                    act.wait_ge(unit_free, t.units_before())
                nc.scalar.activation(o_raw[t.p][:, c, :], o_bank[:, 0:N], ACT.Copy).then_inc(o_saved, 1)

            def step(t):
                for h in range(H):
                    if t.project and h in (2, 4, 6):
                        kq_hi_part(t, ("K01", "K2Q0", "Q12")[h // 2 - 1])
                    if (t.attend and h >= 2) or (t.finish and h < 2):
                        s, hh = t.head(h - 2)
                        if not on_dve(hh):
                            copy_probT(s, hh)
                    if t.attend:
                        exps(t, h)
                    if h == 3 and t.finish:
                        save_o(t.head(-1)[0], 2)
                    if h in (7, 11) and t.attend:
                        save_o(t, h // 4 - 1)

            steps(act, step)

        @block.tensor
        def _(pe):
            def product(ps, w_pair, m_pair):
                n = len(w_pair[0])
                for k in range(n):
                    for e, (a, b) in enumerate(((0, 0), (0, 1), (1, 0))):
                        last = nc.tensor.matmul(ps, w_pair[a][k], m_pair[b][k],
                                                start=(k == 0 and e == 0), stop=(k == n - 1 and e == 2))
                return last

            def claim(t, name):
                if t.looped or t.units_before(name) >= 2:
                    pe.wait_ge(unit_free, t.units_before(name) - 1)
                return shared[t.bank(name)]

            def kq(t, name, part):
                w, c = KQ[name][part]
                q = (t.c + 1) % 2
                bank = claim(t, name)
                if name == "K01" and part == 0:
                    pe.wait_ge(xt_ready, t.count(1, 2))
                if t.c == -1:
                    pe.wait_ge(w_ready, 2)
                last = product(bank[:, N * part:N * (part + 1)],
                               [[a[:, w, k, P * c:P * (c + 1)] for k in range(KC)] for a in (w_hi, w_lo)],
                               [[a[q][:, k, :] for k in range(KC)] for a in (xt_hi, xt_lo)])
                if part:
                    last.then_inc(unit_done, 1)

            def values(t, c):
                q = (t.c + 1) % 2
                bank = claim(t, f"V{c}")
                if t.c == -1:
                    pe.wait_ge(w_ready, 4)
                product(bank[:, 0:D],
                        [[a[q][:, k, P * c:P * (c + 1)] for k in range(KC)] for a in (xt_hi, xt_lo)],
                        [[a[:, W_V, k, :] for k in range(KC)] for a in (w_hi, w_lo)]).then_inc(unit_done, 1)

            def flag(t):
                bank = claim(t, "flag")
                pe.wait_ge(zero_counted, t.count(1))
                nc.tensor.matmul(bank[0:1, 0:1], zero_rows[:], ones[:], start=True, stop=True).then_inc(unit_done, 1)

            def sumT(t):
                bank = claim(t, "sumT")
                pe.wait_ge(inv_ready, t.count(1))
                for c in range(NT):
                    last = nc.tensor.matmul(bank[0:H, P * c:P * (c + 1)], inv[:, c, :], ident[:],
                                            start=True, stop=True)
                last.then_inc(unit_done, 1)

            def spread(t, name):
                bank = claim(t, name)
                pe.wait_ge(unit_free, t.units_before("sumT") + 1)
                for c in ((0, 1) if name == "R01" else (2,)):
                    ps = bank[:, N * (c % 2):N * (c % 2 + 1)]
                    nc.tensor.matmul(ps, sel[:, P * c:P * (c + 1)], inv_hi[:], start=True, stop=False)
                    last = nc.tensor.matmul(ps, sel[:, P * c:P * (c + 1)], inv_lo[:], start=False, stop=True)
                last.then_inc(unit_done, 1)

            def project_out(t, c):
                bank = claim(t, f"Y{c}")
                pe.wait_ge(o_ready, t.count(1))
                product(bank[:, 0:D],
                        [[a[:, k, P * c:P * (c + 1)] for k in range(KC)] for a in (o_hi, o_lo)],
                        [[a[:, W_O, k, :] for k in range(KC)] for a in (w_hi, w_lo)]).then_inc(unit_done, 1)

            def scores(t, h):
                if h % KC == 0:
                    pe.wait_ge(stacked[h // KC], t.count(STACK_DMAS * DMA, STACK_DMAS * DMA))
                if t.looped or t.count(H, h) >= S_BANKS:
                    pe.wait_ge(neg_ready, t.count(H * NT, NT * (h - S_BANKS + 1)))
                for c in range(NT):
                    last = nc.tensor.matmul(s_bank[h % S_BANKS][:, c, :], q_stack[t.p][:, h, P * c:P * (c + 1)],
                                            k_stack[t.p][:, h, :], start=True, stop=True)
                last.then_inc(scored, 1)

            def transposes(t, h):
                pe.wait_ge(prob_ready, t.count(H * NT, NT * (h + 1)))
                if t.looped or t.count(H, h) >= 2:
                    s, hh = t.head(h - 2)
                    if on_dve(hh):
                        pe.wait_ge(probT_dve, dve_heads(s, hh))
                    else:
                        pe.wait_ge(probT_act, act_heads(s, hh))
                for m in range(NT):
                    for c in range(NT):
                        last = nc.tensor.transpose(t_bank[h % 2][:, m, P * c:P * (c + 1)],
                                                   prob[:, h % P_RING, c, P * m:P * (m + 1)], ident[:])
                last.then_inc(transposed, 1)

            def weigh(t, c):
                h = JH * c + JH - 1
                pe.wait_ge(probT_dve, dve_heads(t, h))
                pe.wait_ge(probT_act, act_heads(t, h))
                if c == 0:
                    pe.wait_ge(unit_free, t.units_before())
                if t.looped or t.count(KC, c) >= 1:
                    pe.wait_ge(o_saved, t.count(KC, c))
                for m in range(NT):
                    for j in range(JH):
                        h = JH * c + j
                        last = nc.tensor.matmul(o_bank[HD * j:HD * (j + 1), 0:N], v[t.p][:, m, HD * h:HD * (h + 1)],
                                                probT[:, h % PT_RING, m, :], start=(m == 0), stop=(m == NT - 1))
                last.then_inc(pv_done, 1)

            pe.wait_ge(const_ready, 8)

            def step(t):
                for h in range(H):
                    if t.attend:
                        scores(t, h)
                    if (t.attend and h >= 2) or (t.finish and h < 2):
                        transposes(*t.head(h - 2))
                    if t.finish and h == 0:
                        flag(t)
                    if t.finish and h == 2:
                        sumT(t)
                    if t.project and h < 4:
                        kq(t, ("K01", "K2Q0")[h // 2], h % 2)
                    if t.finish and h == 4:
                        spread(t, "R01")
                        spread(t, "R2")
                    if t.project and h in (4, 5):
                        kq(t, "Q12", h % 2)
                    if t.project and h in (6, 7):
                        values(t, h - 6)
                    if t.finish and h in (8, 9):
                        project_out(t, h - 8)
                    if t.finish and h == 2:
                        weigh(t.head(-1)[0], 2)
                    if t.attend and h in (6, 10):
                        weigh(t, h // 4 - 1)

            steps(pe, step)

        @block.vector
        def _(dve):
            any_zero = dve.alloc_register("any_zero")
            dve.wait_ge(w_loaded, 4 * DMA)
            nc.vector.tensor_scalar(w_f[:, W_Q], w_f[:, W_Q], SCALE, None, ALU.mult).then_inc(w_scaled, 1)
            for k, w in enumerate((W_K, W_Q, W_V, W_O)):
                dve.wait_ge(w_hi_ready, k + 1)
                nc.vector.tensor_tensor(w_lo[:, w], w_f[:, w], w_hi[:, w].bitcast(F32), ALU.subtract
                                        ).then_inc(w_ready, 1)

            def add_bias(t, h):
                dve.wait_ge(scored, t.count(H, h + 1))
                if h == 0:
                    dve.wait_ge(bias_loaded[t.p], DMA * (t.c // 2 + 1) + t.i * DMA)
                if t.looped or t.c >= 1:
                    dve.wait_ge(prob_ready, t.count(H * NT, NT * (h + 1) - H * NT))
                apart(dve)
                for c in range(NT):
                    nc.vector.tensor_tensor_reduce(out=neg[:, h, c], in0=s_bank[h % S_BANKS][:, c, :],
                                                   in1=bias[t.p][:, c, :], scale=-1.0, scalar=BIG,
                                                   op0=ALU.add, op1=ALU.min,
                                                   accum_out=negmax[t.p][:, c, h:h + 1]).then_inc(neg_ready, 1)

            def copy_probT(t, h):
                g = t.count(H, h)
                dve.wait_ge(transposed, g + 1)
                if t.looped or g >= PT_RING:
                    dve.wait_ge(pv_done, t.count(KC, (h - PT_RING) // JH + 1))
                nc.vector.tensor_copy(probT[:, h % PT_RING], t_bank[h % 2][:]).then_inc(probT_dve, 1)

            def kq_lo_part(t, k, name):
                dve.wait_ge(kq_hi_ready, t.count(3, 3 + k + 1))
                a = KQ_AT[name]
                nc.vector.tensor_tensor(kq_lo[:, a:a + 2, :], shared[t.bank(name)][:].rearrange("p (a n) -> p a n", a=2),
                                        kq_hi[:, a:a + 2, :].bitcast(F32), ALU.subtract).then_inc(unit_free, 1)

            def save_v(t, c):
                name = f"V{c}"
                dve.wait_ge(unit_done, t.units_before(name) + 1)
                if c == 0:
                    dve.wait_ge(b_loaded, 2 * DMA)
                    if t.looped or t.c >= 1:
                        dve.wait_ge(pv_done, t.count(KC))
                nc.vector.tensor_tensor(v[(t.c + 1) % 2][:, c, :], shared[t.bank(name)][:, 0:D], bv_all[:], ALU.add
                                        ).then_inc(unit_free, 1)

            def count_zero(t):
                dve.wait_ge(neg_ready, t.count(H * NT, H * NT))
                if t.looped or t.c >= 1:
                    dve.wait_ge(unit_done, t.units_before("flag") + 1)
                nc.vector.tensor_scalar(zero_max[:], negmax[t.p][:], 0.0, 0.0, ALU.is_equal, ALU.add,
                                        accum_out=zero_rows[:]).then_inc(zero_counted, 1)

            def own(t, k):
                dve.wait_ge(dve_step, t.count(DVE_STEPS, k - DVE_STEPS))

            def mask(t):
                nc.vector.memset(keep[:], 1.0).then_inc(dve_step, 1)
                dve.wait_ge(unit_done, t.units_before("flag") + 1)
                nc.vector.tensor_copy(zero_flag[:], shared[t.bank("flag")][0:1, 0:1]).then_inc(unit_free, 1)
                dve.wait_ge(unit_free, t.units_before("flag") + 1)
                dve.wait_ge(zero_counted, t.count(1))
                own(t, 1)
                apart(dve)
                dve.reg_load(any_zero, zero_flag[0:1, 0:1])
                with dve.If_ne(any_zero, 0):
                    nc.vector.tensor_reduce(most[:].rearrange("p c h -> p h c"), neg[:], AX.X, ALU.max)
                    dve.drain()
                    nc.vector.scalar_tensor_tensor(out=keep[:], in0=most[:], scalar=0.0, in1=zero_max[:],
                                                   op0=ALU.is_equal, op1=ALU.mult)
                    dve.drain()
                    nc.vector.tensor_scalar(keep[:], keep[:], -1.0, 1.0, ALU.mult, ALU.add)
                    dve.drain()

            def invert(t):
                p = (t.c + 1) % 2
                dve.wait_ge(prob_ready, t.count(H * NT))
                nc.vector.reciprocal(recip[:], sums[p][:]).then_inc(dve_step, 1)
                own(t, 2)
                nc.vector.tensor_tensor(inv[:], recip[:], keep[:], ALU.mult).then_inc(inv_ready, 1)

            def split_inv(t):
                bank = shared[t.bank("sumT")]
                dve.wait_ge(unit_done, t.units_before("sumT") + 1)
                nc.vector.tensor_copy(inv_hi[:], bank[0:H, 0:N]).then_inc(dve_step, 1)
                own(t, 3)
                nc.vector.tensor_tensor(inv_lo[:], bank[0:H, 0:N], inv_hi[:].bitcast(F32), ALU.subtract
                                        ).then_inc(unit_free, 1)

            def divide(t):
                p = (t.c + 1) % 2
                dve.wait_ge(o_saved, t.count(KC))
                if t.looped or t.c >= 2:
                    dve.wait_ge(o_ready, t.count(1, -1))
                for name, a, b in (("R01", 0, 2), ("R2", 2, 3)):
                    dve.wait_ge(unit_done, t.units_before(name) + 1)
                    nc.vector.tensor_tensor(o_n[:, a:b, :], o_raw[p][:, a:b, :],
                                            shared[t.bank(name)][:, 0:N * (b - a)].rearrange("p (a n) -> p a n", n=N),
                                            ALU.mult).then_inc(unit_free, 1)

            def residual(t, c):
                p = (t.c + 1) % 2
                name = f"Y{c}"
                dve.wait_ge(unit_done, t.units_before(name) + 1)
                dve.wait_ge(xr_ready, t.count(1))
                nc.vector.tensor_tensor(y[:, c, :], shared[t.bank(name)][:, 0:D], xr[p][:, c, :], ALU.add
                                        ).then_inc(unit_free, 1)
                dve.wait_ge(unit_free, t.units_before(name) + 1)
                nc.vector.bn_stats(stats[:, c, :], y[:, c, :]).then_inc(dve_step, 1)
                own(t, 4 + c)
                apart(dve)
                nc.vector.bn_aggr(meanvar[:, c, :], stats[:, c, :]).then_inc(stats_ready, 1)

            def normalise(t):
                dve.wait_ge(rstd_ready, t.count(1))
                if t.looped or t.c >= 2:
                    dve.wait_ge(stored, t.count(DMA, -DMA))
                for c in range(NT):
                    nc.vector.tensor_scalar(y_out[:, c, :], y[:, c, :], meanvar[:, c, 0:1], rstd[:, c:c + 1],
                                            ALU.subtract, ALU.mult).then_inc(y_ready, 1)

            def step(t):
                for h in range(H):
                    if t.finish and h == 0:
                        mask(t)
                    if t.attend:
                        add_bias(t, h)
                    if t.finish and h == 1:
                        invert(t)
                    if (t.attend and h >= 2) or (t.finish and h < 2):
                        s, hh = t.head(h - 2)
                        if on_dve(hh):
                            copy_probT(s, hh)
                    if t.project and h == 2:
                        kq_lo_part(t, 0, "K01")
                    if t.finish and h == 3:
                        split_inv(t)
                    if t.project and h == 4:
                        kq_lo_part(t, 1, "K2Q0")
                    if t.finish and h == 4:
                        divide(t)
                    if t.project and h == 6:
                        kq_lo_part(t, 2, "Q12")
                    if t.project and h in (7, 8):
                        save_v(t, h - 7)
                    if t.finish and h in (9, 10):
                        residual(t, h - 9)
                    if t.finish and h == 11:
                        normalise(t)
                if t.attend:
                    count_zero(t)

            steps(dve, step)


_INS = ["x", "xT", "adj", "wqT", "wkT", "wvT", "bv", "woT", "bo"]


def kernel(x, adj, L0_gnn_Wq, L0_gnn_Wk, L0_gnn_Wv, L0_gnn_bv, L0_gnn_Wo, L0_gnn_bo):
    import numpy as np
    import concourse.bacc as bacc
    from concourse.bass_utils import run_bass_kernel_spmd

    def grouped(w):
        return np.asarray(w).reshape(JH, KC, HD, D).transpose(3, 1, 0, 2).reshape(D, D)

    arrays = {
        "x": np.asarray(x), "xT": np.asarray(x).transpose(0, 2, 1), "adj": np.asarray(adj),
        "wqT": grouped(L0_gnn_Wq), "wkT": grouped(L0_gnn_Wk), "wvT": np.asarray(L0_gnn_Wv).T,
        "bv": np.asarray(L0_gnn_bv), "woT": np.asarray(L0_gnn_Wo).T, "bo": np.asarray(L0_gnn_bo),
    }
    arrays = {k: np.ascontiguousarray(a) for k, a in arrays.items()}
    nc = bacc.Bacc("TRN2", target_bir_lowering=False, num_devices=1)
    args = [nc.dram_tensor(f"in_{k}", arrays[k].shape, mybir.dt.from_np(arrays[k].dtype), kind="ExternalInput").ap()
            for k in _INS]
    y = nc.dram_tensor("out_y", (B, N, D), F32, kind="ExternalOutput").ap()
    build(nc, *args, y)
    r = run_bass_kernel_spmd(nc, [{f"in_{k}": arrays[k] for k in _INS}], core_ids=[0])
    return r.results[0]["out_y"]
```

```python
import concourse.bass as bass
from concourse import mybir

F32 = mybir.dt.float32
F32R = mybir.dt.float32r
BF16 = mybir.dt.bfloat16
I32 = mybir.dt.int32
ALU = mybir.AluOpType
ACT = mybir.ActivationFunctionType
AX = mybir.AxisListType

B, N, D = 32, 256, 384
H, HD = 12, 32
P = 128
KC = D // P
NT = N // P
JH = P // HD
SCALE = D ** -0.5
EPS = 1e-5
BIG = 3.0e38

S_BANKS, P_RING, PT_RING = 2, 4, 6
DMA = 16
STACK_DMAS = 6
HALF = H // 2

PROJECT, FINISH = ("K01", "K2Q0", "Q12", "V0", "V1"), ("sumT", "R01", "R2", "Y0", "Y1")
BANK = {"K01": 0, "sumT": 2, "K2Q0": 1, "R01": 2, "R2": 1, "Q12": 0, "V0": 2, "V1": 1, "Y0": 0, "Y1": 2}
PLAN = [
    [("K01", 0, 4)],
    [("K01", 4, 6), ("K2Q0", 0, 1)],
    [("K2Q0", 1, 3)],
    [("K2Q0", 3, 5), ("sumT", 0, 1), ("K2Q0", 5, 6)],
    [("Q12", 0, 3)],
    [("R01", 0, 1), ("Q12", 3, 5), ("R2", 0, 1), ("Q12", 5, 6)],
    [("V0", 0, 1)],
    [("V0", 1, 3), ("V1", 0, 1)],
    [("V1", 1, 3)],
    [("Y0", 0, 3)],
    [],
    [("Y1", 0, 3)],
]


class Step:

    def __init__(self, i, c):
        self.i, self.c, self.n, self.p = i, c, 2 * i + c, c % 2
        looped = not isinstance(i, int)
        self.attend = looped or 0 <= c < B
        self.finish = looped or 1 <= c <= B
        self.project = looped or -1 <= c <= B - 2
        self.looped = looped

    def count(self, per_step, extra=0):
        return self.i * (2 * per_step) + (self.c * per_step + extra)

    def units(self):
        return [u for u in BANK if (u in PROJECT and self.project) or (u in FINISH and self.finish)]

    def units_before(self, name=None):
        k = 0 if name is None else self.units().index(name)
        if not self.looped and not 1 <= self.c < B:
            return {-1: 0, 0: len(PROJECT), B: len(BANK) * (B - 1) + len(BANK) // 2}[self.c] + k
        return self.count(len(BANK), k)

    def before(self):
        return Step(self.i, self.c - 1)

    def last_user(self, name):
        order = self.units()
        mine = [u for u in order[:order.index(name)] if BANK[u] == BANK[name]]
        if mine:
            return self.units_before(mine[-1]) + 1
        t = self.before()
        while t.looped or t.c >= -1:
            users = [u for u in t.units() if BANK[u] == BANK[name]]
            if users:
                return t.units_before(users[-1]) + 1
            t = t.before()
        return None

    def head(self, h):
        return (self, h) if h >= 0 else (self.before(), h + H)


def plan(t, h):
    if t.c == B - 1 and h in (9, 11):
        return PLAN[9] + PLAN[11] if h == 11 else []
    return [w for w in PLAN[h] if w[0] in t.units()]


def on_dve(h):
    return h % 3 == 1


def dve_heads(t, h):
    return t.count(H // 3, (h + 2) // 3)


def act_heads(t, h):
    return t.count(H - H // 3, h + 1 - (h + 2) // 3)


def steps(eng, body):
    for c in range(-1, 3):
        body(Step(0, c))
    with eng.Fori(1, (B - 4) // 2) as i:
        body(Step(i, 1))
        body(Step(i, 2))
    for c in range(B - 3, B + 2):
        body(Step(0, c))


def build(nc, x, xT, adj, wqT, wkT, wvT, bv, woT, bo, out):
    def sb(name, shape, dt=F32):
        return nc.alloc_sbuf_tensor(name, shape, dt)

    ident = sb("ident", [P, P])
    ones = sb("ones", [P, P], BF16)
    sel_f = sb("sel_f", [HD + H, D])
    sel = sb("sel", [HD + H, D], F32R)
    halfs = sb("halfs", [P, NT])
    w_hi = sb("w_hi", [P, 4, KC, D], F32R)
    w_lo = sb("w_lo", [P, 4, KC, D], F32R)
    bv_all = sb("bv_all", [P, D])
    bo_all = sb("bo_all", [P, D])
    xt = [sb(f"xt{p}", [P, KC, N]) for p in range(2)]
    xt_hi = [sb(f"xt_hi{p}", [P, KC, N], F32R) for p in range(2)]
    xt_lo = [sb(f"xt_lo{p}", [P, KC, N], F32R) for p in range(2)]
    xr = [sb(f"xr{p}", [P, NT, D]) for p in range(2)]
    bias = [sb(f"bias{p}", [P, NT, N]) for p in range(2)]
    kq_hi = sb("kq_hi", [P, 2 * KC, N], F32R)
    kq_lo = sb("kq_lo", [P, 2 * KC, N], F32R)
    k_stack = [sb(f"k_stack{p}", [3 * HD, H, N], F32R) for p in range(2)]
    q_stack = [sb(f"q_stack{p}", [3 * HD, H, N], F32R) for p in range(2)]
    v = [sb(f"v{p}", [P, NT, D]) for p in range(2)]
    neg = sb("neg", [P, H, NT, N])
    w_f = (neg[:, 0:4 * KC * D // (NT * N)].rearrange("p h c n -> p (h c n)")
           .rearrange("p (w k d) -> p w k d", w=4, k=KC))
    negmax = [sb(f"negmax{p}", [P, NT, H]) for p in range(2)]
    sums = [sb(f"sums{p}", [P, NT, H]) for p in range(2)]
    prob = sb("prob", [P, P_RING, NT, N])
    probT = sb("probT", [P, PT_RING, NT, N])
    zero_max = [sb(f"zero_max{g}", [P, NT, HALF], BF16) for g in range(2)]
    zero_flag = sb("zero_flag", [1, 1], I32)
    most = sb("most", [P, NT, H])
    keep = sb("keep", [P, NT, H])
    recip = sb("recip", [P, NT, H])
    inv = sb("inv", [P, NT, H])
    inv_t = sb("inv_t", [HD + H, N], F32R)
    o_raw = [sb(f"o_raw{p}", [P, KC, N]) for p in range(2)]
    o_n = sb("o_n", [P, KC, N])
    o_hi = sb("o_hi", [P, KC, N], F32R)
    o_lo = sb("o_lo", [P, KC, N], F32R)
    y = sb("y", [P, NT, D])
    stats = sb("stats", [P, NT, 6])
    meanvar = sb("meanvar", [P, NT, 2])
    var_eps = sb("var_eps", [P, NT])
    rstd = sb("rstd", [P, NT])
    y_out = sb("y_out", [P, NT, D])

    s_bank = [nc.alloc_psum_tensor(f"s_bank{k}", [P, NT, N], F32) for k in range(S_BANKS)]
    t_bank = [nc.alloc_psum_tensor(f"t_bank{k}", [P, NT, N], F32) for k in range(2)]
    o_bank = nc.alloc_psum_tensor("o_bank", [P, NT * N], F32)
    shared = [nc.alloc_psum_tensor(f"shared{k}", [P, NT * N], F32) for k in range(3)]
    flags_at = o_bank[:, N:N + NT * HALF]

    sem = nc.alloc_semaphore
    const_ready = sem("const_ready")
    w_loaded = [sem(f"w_loaded{w}") for w in "qkvo"]
    b_loaded = sem("b_loaded")
    w_hi_ready = sem("w_hi_ready")
    w_ready = sem("w_ready")
    xt_loaded = [sem(f"xt_loaded{p}") for p in range(2)]
    xr_loaded = [sem(f"xr_loaded{p}") for p in range(2)]
    bias_loaded = [sem(f"bias_loaded{p}") for p in range(2)]
    xt_hi_ready = sem("xt_hi_ready")
    xt_ready = sem("xt_ready")
    xr_ready = sem("xr_ready")
    kq_hi_ready = sem("kq_hi_ready")
    stacked = sem("stacked")
    scored = sem("scored")
    neg_ready = sem("neg_ready")
    prob_ready = sem("prob_ready")
    transposed = sem("transposed")
    probT_dve = sem("probT_dve")
    probT_act = sem("probT_act")
    pv_done = sem("pv_done")
    o_saved = sem("o_saved")
    unit_done = sem("unit_done")
    unit_free = sem("unit_free")
    zero_found = sem("zero_found")
    flag_done = sem("flag_done")
    flag_read = sem("flag_read")
    keep_set = sem("keep_set")
    recip_ready = sem("recip_ready")
    inv_hi_ready = sem("inv_hi_ready")
    bn_ready = sem("bn_ready")
    inv_ready = sem("inv_ready")
    o_hi_ready = sem("o_hi_ready")
    o_ready = sem("o_ready")
    stats_ready = sem("stats_ready")
    var_ready = sem("var_ready")
    rstd_ready = sem("rstd_ready")
    y_ready = sem("y_ready")
    stored = sem("stored")
    passed = sem("passed")

    W_Q, W_K, W_V, W_O = range(4)
    KQ = {"K01": [(W_K, 0), (W_K, 1)], "K2Q0": [(W_K, 2), (W_Q, 0)], "Q12": [(W_Q, 1), (W_Q, 2)]}
    KQ_AT = {"K01": 0, "K2Q0": 2, "Q12": 4}

    def apart(eng):
        eng.sem_inc(passed, 1)

    with nc.Block() as block:

        @block.sync
        def _(sp):
            def load_xt(t, k):
                sp.dma_start(xt[(t.c + k) % 2][:], xT[t.n + k].rearrange("(c p) n -> p c n", p=P)
                             ).then_inc(xt_loaded[(t.c + k) % 2], DMA)

            load_xt(Step(0, 0), 0)
            for w, src in ((W_K, wkT), (W_Q, wqT), (W_V, wvT), (W_O, woT)):
                sp.dma_start(w_f[:, w], src.rearrange("(c p) n -> p c n", p=P)).then_inc(w_loaded[w], DMA)
            load_xt(Step(0, 0), 1)
            for dst, src in ((bv_all, bv), (bo_all, bo)):
                sp.dma_start(dst[:], src.rearrange("(a n) -> a n", a=1).to_broadcast([P, D])
                             ).then_inc(b_loaded, DMA)

            def stack(t, k):
                dst = (k_stack, q_stack)[k][(t.c + 1) % 2]
                for r, part in enumerate(((kq_hi, kq_hi, kq_lo), (kq_hi, kq_lo, kq_hi))[k]):
                    sp.dma_start(dst[HD * r:HD * (r + 1)].rearrange("d (j c) n -> d j c n", j=JH).bitcast(F32),
                                 part[:, KC * k:KC * (k + 1), :].bitcast(F32)).then_inc(stacked, DMA)

            def step(t):
                if t.looped or t.c <= B - 4:
                    sp.wait_ge(xt_ready, t.count(1, 2))
                    load_xt(t, 3)
                if t.project:
                    q = (t.c + 1) % 2
                    if t.looped or t.c >= 1:
                        sp.wait_ge(neg_ready, t.count(H * NT))
                    sp.dma_start(bias[q][:], adj[t.n + 1].rearrange("(c p) m -> p c m", p=P)
                                 ).then_inc(bias_loaded[q], DMA)
                if t.attend:
                    if t.looped or t.c >= 2:
                        sp.wait_ge(unit_free, t.units_before())
                    sp.dma_start(xr[t.p][:], x[t.n].rearrange("(c p) d -> p c d", p=P)
                                 ).then_inc(xr_loaded[t.p], DMA)
                if t.project:
                    if t.looped or t.c >= 1:
                        sp.wait_ge(scored, t.count(H))
                        apart(sp)
                    sp.wait_ge(kq_hi_ready, t.count(3, 3 + 2))
                    apart(sp)
                    sp.wait_ge(unit_free, t.units_before("K2Q0") + 1)
                    stack(t, 0)
                    sp.wait_ge(kq_hi_ready, t.count(3, 3 + 3))
                    apart(sp)
                    sp.wait_ge(unit_free, t.units_before("Q12") + 1)
                    stack(t, 1)
                if t.before().finish:
                    sp.wait_ge(y_ready, t.count(NT, -NT))
                    sp.dma_start(out[t.n - 2].rearrange("(c p) d -> p c d", p=P), y_out[:]
                                 ).then_inc(stored, DMA)

            steps(sp, step)
            sp.wait_ge(stored, DMA * B)

        @block.gpsimd
        def _(pool):
            nc.gpsimd.memset(ident[:], 0.0).then_inc(const_ready, 1)
            nc.gpsimd.memset(sel_f[:], 1.0).then_inc(const_ready, 1)
            nc.gpsimd.memset(ones[:], 1.0).then_inc(const_ready, 1)
            nc.gpsimd.memset(halfs[:], -0.5).then_inc(const_ready, 1)
            nc.gpsimd.memset(inv_t[:].bitcast(F32), 0.0).then_inc(const_ready, 1)
            pool.wait_ge(const_ready, 5)
            nc.gpsimd.affine_select(out=ident[:], in_=ident[:], compare_op=ALU.not_equal, fill=1.0,
                                    base=0, pattern=[[-1, P]], channel_multiplier=1).then_inc(const_ready, 1)
            for k, (at, n) in enumerate(((0, HD), (HD, H))):
                rows = sel_f[at:at + n, :]
                pool.wait_ge(const_ready, 6 + 2 * k)
                nc.gpsimd.affine_select(out=rows, in_=rows, compare_op=ALU.is_ge, fill=0.0,
                                        base=0, pattern=[[1, D]], channel_multiplier=-HD).then_inc(const_ready, 1)
                pool.wait_ge(const_ready, 7 + 2 * k)
                nc.gpsimd.affine_select(out=rows, in_=rows, compare_op=ALU.is_ge, fill=0.0,
                                        base=HD - 1, pattern=[[-1, D]], channel_multiplier=HD).then_inc(const_ready, 1)
            pool.wait_ge(const_ready, 10)
            nc.gpsimd.tensor_copy(sel[:], sel_f[:]).then_inc(const_ready, 1)

            def split_xt(t, k):
                q = (t.c + k) % 2
                pool.wait_ge(xt_loaded[q], DMA * ((t.c + k) // 2 + 1) + t.i * DMA)
                apart(pool)
                nc.gpsimd.tensor_copy(xt_hi[q][:], xt[q][:]).then_inc(xt_hi_ready, 1)
                pool.wait_ge(xt_hi_ready, t.count(1, k + 1))
                nc.gpsimd.tensor_tensor(xt_lo[q][:], xt[q][:], xt_hi[q][:].bitcast(F32), ALU.subtract
                                        ).then_inc(xt_ready, 1)

            def step(t):
                if t.c == -1:
                    pool.wait_ge(xt_ready, 1)
                if t.looped or t.c <= B - 3:
                    if t.looped or t.c >= 0:
                        pool.wait_ge(unit_done, t.units_before())
                    split_xt(t, 2)
                if t.before().finish:
                    pool.wait_ge(stats_ready, t.count(NT, -NT))
                    apart(pool)
                    nc.gpsimd.tensor_scalar(var_eps[:], meanvar[:, :, 1], EPS, None, ALU.add
                                            ).then_inc(var_ready, 1)
                    pool.wait_ge(var_ready, t.count(1, -1))
                    nc.gpsimd.tensor_tensor(rstd[:], var_eps[:], halfs[:], ALU.pow).then_inc(rstd_ready, 1)
                if t.attend:
                    pool.wait_ge(b_loaded, 2 * DMA)
                    pool.wait_ge(xr_loaded[t.p], DMA * (t.c // 2 + 1) + t.i * DMA)
                    nc.gpsimd.tensor_tensor(xr[t.p][:], xr[t.p][:], bo_all[:].unsqueeze(1).to_broadcast([P, NT, D]),
                                            ALU.add).then_inc(xr_ready, 1)
                if t.finish:
                    pool.wait_ge(unit_free, t.units_before("R2") + 1)
                    if t.looped or t.c >= 2:
                        pool.wait_ge(unit_done, t.units_before())
                    pool.wait_ge(o_hi_ready, t.count(1))
                    nc.gpsimd.tensor_tensor(o_lo[:], o_n[:], o_hi[:].bitcast(F32), ALU.subtract
                                            ).then_inc(o_ready, 1)

            steps(pool, step)

        @block.scalar
        def _(act):
            for w in (W_K, W_Q, W_V, W_O):
                act.wait_ge(w_loaded[w], DMA)
                nc.scalar.activation(w_hi[:, w], w_f[:, w], ACT.Copy, scale=SCALE if w == W_Q else 1.0
                                     ).then_inc(w_hi_ready, 1)

            def kq_hi_part(t, name):
                act.wait_ge(unit_done, t.units_before(name) + 1)
                if name == "K01" and (t.looped or t.c >= 0):
                    act.wait_ge(stacked, t.count(STACK_DMAS * DMA, STACK_DMAS * DMA))
                a = KQ_AT[name]
                nc.scalar.activation(kq_hi[:, a:a + 2, :], shared[BANK[name]][:].rearrange("p (a n) -> p a n", a=2),
                                     ACT.Copy).then_inc(kq_hi_ready, 1)

            def copy_probT(t, h):
                g = t.count(H, h)
                act.wait_ge(transposed, g + 1)
                if t.looped or g >= PT_RING:
                    act.wait_ge(pv_done, t.count(KC, (h - PT_RING) // JH + 1))
                nc.scalar.activation(probT[:, h % PT_RING], t_bank[h % 2][:], ACT.Copy).then_inc(probT_act, 1)

            def exps(t, h):
                g = t.count(H, h)
                if t.looped or g >= P_RING:
                    act.wait_ge(transposed, g - P_RING + 1)
                for c in range(NT):
                    act.wait_ge(neg_ready, t.count(H * NT, NT * h + c + 1))
                    if h == 0 and (t.looped or t.c >= 2):
                        act.wait_ge(inv_ready, t.count(1, -1))
                    nc.scalar.activation(prob[:, h % P_RING, c], neg[:, h, c], ACT.Exp, scale=-1.0,
                                         bias=negmax[t.p][:, c, h:h + 1], accum_out=sums[t.p][:, c, h:h + 1]
                                         ).then_inc(prob_ready, 1)

            def split_o(t):
                act.wait_ge(unit_free, t.units_before("R2") + 1)
                if t.looped or t.c >= 2:
                    act.wait_ge(unit_done, t.units_before())
                nc.scalar.activation(o_hi[:], o_n[:], ACT.Copy).then_inc(o_hi_ready, 1)

            def save_o(t, c):
                act.wait_ge(pv_done, t.count(KC, c + 1))
                if c == 0 and (t.looped or t.c >= 2):
                    act.wait_ge(unit_free, t.units_before())
                nc.scalar.activation(o_raw[t.p][:, c, :], o_bank[:, 0:N], ACT.Copy).then_inc(o_saved, 1)

            def step(t):
                for h in range(H):
                    if t.project and h in (2, 4, 6):
                        kq_hi_part(t, ("K01", "K2Q0", "Q12")[h // 2 - 1])
                    if (t.attend and h >= 2) or (t.finish and h < 2):
                        s, hh = t.head(h - 2)
                        if not on_dve(hh):
                            copy_probT(s, hh)
                    if t.attend:
                        exps(t, h)
                    if h == 3 and t.finish:
                        save_o(t.head(-1)[0], 2)
                    if h in (7, 11) and t.attend:
                        save_o(t, h // 4 - 1)
                    if h == 6 and t.finish:
                        split_o(t)

            steps(act, step)

        @block.tensor
        def _(pe):
            def product(ps, w_pair, m_pair, k):
                for e, (a, b) in enumerate(((0, 0), (0, 1), (1, 0))):
                    last = nc.tensor.matmul(ps, w_pair[a](k), m_pair[b](k),
                                            start=(k == 0 and e == 0), stop=(k == KC - 1 and e == 2))
                return last

            def unit(t, name, first, end):
                bank = shared[BANK[name]]
                q = (t.c + 1) % 2
                if first == 0:
                    used = t.last_user(name)
                    if used is not None:
                        pe.wait_ge(unit_free, used)
                    if name == "K01":
                        pe.wait_ge(xt_ready, t.count(1, 2))
                    if t.c == -1:
                        pe.wait_ge(w_ready, {"K01": 1, "K2Q0": 2, "Q12": 2, "V0": 4, "V1": 4}[name])
                    if name == "sumT":
                        pe.wait_ge(inv_ready, t.count(1))
                    if name in ("R01", "R2"):
                        pe.wait_ge(unit_free, t.units_before("sumT") + 1)
                    if name == "Y0":
                        pe.wait_ge(o_ready, t.count(1))
                for piece in range(first, end):
                    k = piece % KC
                    if name in KQ:
                        part = piece // KC
                        w, c = KQ[name][part]
                        last = product(bank[:, N * part:N * (part + 1)],
                                       [lambda k, a=a: a[:, w, k, P * c:P * (c + 1)] for a in (w_hi, w_lo)],
                                       [lambda k, a=a: a[q][:, k, :] for a in (xt_hi, xt_lo)], k)
                        ends = piece == 2 * KC - 1
                    elif name == "sumT":
                        for c in range(NT):
                            last = nc.tensor.matmul(bank[0:H, P * c:P * (c + 1)], inv[:, c, :], ident[:],
                                                    start=True, stop=True)
                        ends = True
                    elif name in ("R01", "R2"):
                        for c in ((0, 1) if name == "R01" else (2,)):
                            ps = bank[:, N * (c % 2):N * (c % 2 + 1)]
                            last = nc.tensor.matmul(ps, sel[:, P * c:P * (c + 1)], inv_t[:], start=True, stop=True)
                        ends = True
                    else:
                        c = int(name[1])
                        src = [lambda k, a=a: a[:, k, P * c:P * (c + 1)]
                               for a in ((xt_hi[q], xt_lo[q]) if name[0] == "V" else (o_hi, o_lo))]
                        w = W_V if name[0] == "V" else W_O
                        last = product(bank[:, 0:D], src, [lambda k, a=a: a[:, w, k, :] for a in (w_hi, w_lo)], k)
                        ends = k == KC - 1
                if ends:
                    last.then_inc(unit_done, 1)

            def flag(t, g):
                pe.wait_ge(zero_found, t.count(2, g + 1))
                pe.wait_ge(o_saved, t.count(KC, g + 1))
                nc.tensor.matmul(flags_at, ones[:], zero_max[g][:], start=True, stop=True).then_inc(flag_done, 1)

            def scores(t, h):
                if h == 0:
                    pe.wait_ge(stacked, t.count(STACK_DMAS * DMA, STACK_DMAS * DMA))
                if t.looped or t.count(H, h) >= S_BANKS:
                    pe.wait_ge(neg_ready, t.count(H * NT, NT * (h - S_BANKS + 1)))
                for c in range(NT):
                    last = nc.tensor.matmul(s_bank[h % S_BANKS][:, c, :], q_stack[t.p][:, h, P * c:P * (c + 1)],
                                            k_stack[t.p][:, h, :], start=True, stop=True)
                last.then_inc(scored, 1)

            def transposes(t, h):
                pe.wait_ge(prob_ready, t.count(H * NT, NT * (h + 1)))
                if t.looped or t.count(H, h) >= 2:
                    s, hh = t.head(h - 2)
                    if on_dve(hh):
                        pe.wait_ge(probT_dve, dve_heads(s, hh))
                    else:
                        pe.wait_ge(probT_act, act_heads(s, hh))
                for m in range(NT):
                    for c in range(NT):
                        last = nc.tensor.transpose(t_bank[h % 2][:, m, P * c:P * (c + 1)],
                                                   prob[:, h % P_RING, c, P * m:P * (m + 1)], ident[:])
                last.then_inc(transposed, 1)

            def weigh(t, c):
                h = JH * c + JH - 1
                pe.wait_ge(probT_dve, dve_heads(t, h))
                pe.wait_ge(probT_act, act_heads(t, h))
                if c == 0:
                    pe.wait_ge(unit_free, t.units_before())
                if t.looped or t.count(KC, c) >= 1:
                    pe.wait_ge(o_saved, t.count(KC, c))
                if t.looped or t.count(2, c) >= 1:
                    pe.wait_ge(flag_read, t.count(2, c))
                for m in range(NT):
                    for j in range(JH):
                        h = JH * c + j
                        last = nc.tensor.matmul(o_bank[HD * j:HD * (j + 1), 0:N], v[t.p][:, m, HD * h:HD * (h + 1)],
                                                probT[:, h % PT_RING, m, :], start=(m == 0), stop=(m == NT - 1))
                last.then_inc(pv_done, 1)

            pe.wait_ge(const_ready, 11)

            def step(t):
                for h in range(H):
                    if t.attend:
                        scores(t, h)
                    if (t.attend and h >= 2) or (t.finish and h < 2):
                        transposes(*t.head(h - 2))
                    if h in (6, 10) and t.attend:
                        weigh(t, h // 4 - 1)
                    for name, first, end in plan(t, h):
                        unit(t, name, first, end)
                    if h == 2 and t.finish:
                        weigh(t.before(), 2)
                    if h == 0 and t.finish:
                        flag(t.before(), 1)
                    if h == 8 and t.attend:
                        flag(t, 0)

            steps(pe, step)

        @block.vector
        def _(dve):
            any_zero = dve.alloc_register("any_zero")
            dve.wait_ge(xt_loaded[0], DMA)
            nc.vector.tensor_copy(xt_hi[0][:], xt[0][:]).then_inc(xt_hi_ready, 1)
            dve.wait_ge(xt_hi_ready, 1)
            nc.vector.tensor_tensor(xt_lo[0][:], xt[0][:], xt_hi[0][:].bitcast(F32), ALU.subtract
                                    ).then_inc(xt_ready, 1)
            for k, w in enumerate((W_K, W_Q, W_V, W_O)):
                dve.wait_ge(w_hi_ready, k + 1)
                nc.vector.scalar_tensor_tensor(out=w_lo[:, w], in0=w_f[:, w], scalar=SCALE if w == W_Q else 1.0,
                                               in1=w_hi[:, w].bitcast(F32), op0=ALU.mult, op1=ALU.subtract
                                               ).then_inc(w_ready, 1)

            def add_bias(t, h):
                dve.wait_ge(scored, t.count(H, h + 1))
                if h == 0:
                    dve.wait_ge(bias_loaded[t.p], DMA * (t.c // 2 + 1) + t.i * DMA)
                if t.looped or t.c >= 1:
                    dve.wait_ge(prob_ready, t.count(H * NT, NT * (h + 1) - H * NT))
                apart(dve)
                for c in range(NT):
                    nc.vector.tensor_tensor_reduce(out=neg[:, h, c], in0=s_bank[h % S_BANKS][:, c, :],
                                                   in1=bias[t.p][:, c, :], scale=-1.0, scalar=BIG,
                                                   op0=ALU.add, op1=ALU.min,
                                                   accum_out=negmax[t.p][:, c, h:h + 1]).then_inc(neg_ready, 1)

            def copy_probT(t, h):
                g = t.count(H, h)
                dve.wait_ge(transposed, g + 1)
                if t.looped or g >= PT_RING:
                    dve.wait_ge(pv_done, t.count(KC, (h - PT_RING) // JH + 1))
                nc.vector.tensor_copy(probT[:, h % PT_RING], t_bank[h % 2][:]).then_inc(probT_dve, 1)

            def kq_lo_part(t, k, name):
                dve.wait_ge(kq_hi_ready, t.count(3, 3 + k + 1))
                a = KQ_AT[name]
                nc.vector.tensor_tensor(kq_lo[:, a:a + 2, :], shared[BANK[name]][:].rearrange("p (a n) -> p a n", a=2),
                                        kq_hi[:, a:a + 2, :].bitcast(F32), ALU.subtract).then_inc(unit_free, 1)

            def save_v(t, c):
                name = f"V{c}"
                dve.wait_ge(unit_done, t.units_before(name) + 1)
                if c == 0:
                    dve.wait_ge(b_loaded, 2 * DMA)
                    if t.looped or t.c >= 1:
                        dve.wait_ge(pv_done, t.count(KC))
                nc.vector.tensor_tensor(v[(t.c + 1) % 2][:, c, :], shared[BANK[name]][:, 0:D], bv_all[:], ALU.add
                                        ).then_inc(unit_free, 1)

            def find_zero(t, g):
                dve.wait_ge(neg_ready, t.count(H * NT, NT * HALF * (g + 1)))
                if t.looped or t.c >= 1:
                    dve.wait_ge(flag_done, t.count(2, g - 1))
                heads = slice(HALF * g, HALF * (g + 1))
                nc.vector.tensor_scalar(zero_max[g][:], negmax[t.p][:, :, heads], 0.0, None, ALU.is_equal
                                        ).then_inc(zero_found, 1)

            def read_flag(t, g):
                if g == 0:
                    if t.looped or t.c >= 1:
                        dve.wait_ge(inv_ready, t.count(1))
                    nc.vector.memset(keep[:], 1.0).then_inc(keep_set, 1)
                dve.wait_ge(flag_done, t.count(2, g + 1))
                nc.vector.tensor_reduce(zero_flag[:], flags_at[0:1, :], AX.X, ALU.max).then_inc(flag_read, 1)

            def mask(t, g):
                heads = slice(HALF * g, HALF * (g + 1))
                dve.wait_ge(flag_read, t.count(2, g + 1))
                dve.wait_ge(zero_found, t.count(2, g + 1))
                dve.wait_ge(keep_set, t.count(1, 1))
                apart(dve)
                dve.reg_load(any_zero, zero_flag[0:1, 0:1])
                with dve.If_ne(any_zero, 0):
                    nc.vector.tensor_reduce(most[:, :, heads].rearrange("p c h -> p h c"), neg[:, heads], AX.X, ALU.max)
                    dve.drain()
                    nc.vector.scalar_tensor_tensor(out=keep[:, :, heads], in0=most[:, :, heads], scalar=0.0,
                                                   in1=zero_max[g][:], op0=ALU.is_equal, op1=ALU.mult)
                    dve.drain()
                    nc.vector.tensor_scalar(keep[:, :, heads], keep[:, :, heads], -1.0, 1.0, ALU.mult, ALU.add)
                    dve.drain()

            def invert(t):
                p = (t.c + 1) % 2
                dve.wait_ge(prob_ready, t.count(H * NT))
                nc.vector.reciprocal(recip[:], sums[p][:]).then_inc(recip_ready, 1)
                if t.looped or t.c >= 2:
                    dve.wait_ge(unit_done, t.before().units_before("sumT") + 1)
                dve.wait_ge(recip_ready, t.count(1))
                nc.vector.tensor_tensor(inv[:], recip[:], keep[:], ALU.mult).then_inc(inv_ready, 1)

            def split_inv(t):
                bank = shared[BANK["sumT"]]
                dve.wait_ge(unit_done, t.units_before("sumT") + 1)
                dve.wait_ge(const_ready, 11)
                nc.vector.tensor_copy(inv_t[0:H, :], bank[0:H, 0:N]).then_inc(inv_hi_ready, 1)
                dve.wait_ge(inv_hi_ready, t.count(1))
                nc.vector.tensor_tensor(inv_t[HD:HD + H, :], bank[0:H, 0:N], inv_t[0:H, :].bitcast(F32), ALU.subtract
                                        ).then_inc(unit_free, 1)

            def divide(t):
                p = (t.c + 1) % 2
                dve.wait_ge(o_saved, t.count(KC))
                if t.looped or t.c >= 2:
                    dve.wait_ge(o_ready, t.count(1, -1))
                for name, a, b in (("R01", 0, 2), ("R2", 2, 3)):
                    dve.wait_ge(unit_done, t.units_before(name) + 1)
                    nc.vector.tensor_tensor(o_n[:, a:b, :], o_raw[p][:, a:b, :],
                                            shared[BANK[name]][:, 0:N * (b - a)].rearrange("p (a n) -> p a n", n=N),
                                            ALU.mult).then_inc(unit_free, 1)

            def residual(t, c):
                p = (t.c + 1) % 2
                name = f"Y{c}"
                dve.wait_ge(unit_done, t.units_before(name) + 1)
                dve.wait_ge(xr_ready, t.count(1))
                if c == 0 and t.before().finish:
                    dve.wait_ge(y_ready, t.count(NT, -NT))
                nc.vector.tensor_tensor(y[:, c, :], shared[BANK[name]][:, 0:D], xr[p][:, c, :], ALU.add
                                        ).then_inc(unit_free, 1)
                dve.wait_ge(unit_free, t.units_before(name) + 1)
                nc.vector.bn_stats(stats[:, c, :], y[:, c, :]).then_inc(bn_ready, 1)
                dve.wait_ge(bn_ready, t.count(NT, c + 1 - NT))
                apart(dve)
                nc.vector.bn_aggr(meanvar[:, c, :], stats[:, c, :]).then_inc(stats_ready, 1)

            def normalise(t):
                dve.wait_ge(rstd_ready, t.count(1))
                if t.looped or t.c >= 2:
                    dve.wait_ge(stored, t.count(DMA, -DMA))
                for c in range(NT):
                    nc.vector.tensor_scalar(y_out[:, c, :], y[:, c, :], meanvar[:, c, 0:1], rstd[:, c:c + 1],
                                            ALU.subtract, ALU.mult).then_inc(y_ready, 1)

            def step(t):
                for h in range(H):
                    if t.attend:
                        add_bias(t, h)
                    if (t.attend and h >= 2) or (t.finish and h < 2):
                        s, hh = t.head(h - 2)
                        if on_dve(hh):
                            copy_probT(s, hh)
                    if h == 0 and t.before().finish:
                        residual(t.before(), 1)
                    if h == 0 and t.finish:
                        read_flag(t.before(), 1)
                    if h == 1 and t.finish:
                        mask(t.before(), 1)
                    if h == 2 and t.finish:
                        invert(t)
                    if h == 2 and t.project:
                        kq_lo_part(t, 0, "K01")
                    if h == 4 and t.project:
                        kq_lo_part(t, 1, "K2Q0")
                    if h == 3 and t.finish:
                        split_inv(t)
                    if h == 5 and t.finish:
                        divide(t)
                    if h == 6 and t.project:
                        kq_lo_part(t, 2, "Q12")
                    if h == 6 and t.attend:
                        find_zero(t, 0)
                    if h == 7 and t.before().finish:
                        normalise(t.before())
                    if h in (8, 9) and t.project:
                        save_v(t, h - 8)
                    if h == 9 and t.attend:
                        read_flag(t, 0)
                        mask(t, 0)
                    if h == (11 if t.c == B - 1 else 10) and t.finish:
                        residual(t, 0)
                if t.attend:
                    find_zero(t, 1)

            steps(dve, step)


_INS = ["x", "xT", "adj", "wqT", "wkT", "wvT", "bv", "woT", "bo"]


def kernel(x, adj, L0_gnn_Wq, L0_gnn_Wk, L0_gnn_Wv, L0_gnn_bv, L0_gnn_Wo, L0_gnn_bo):
    import numpy as np
    import concourse.bacc as bacc
    from concourse.bass_utils import run_bass_kernel_spmd

    def grouped(w):
        return np.asarray(w).reshape(JH, KC, HD, D).transpose(3, 1, 2, 0).reshape(D, D)

    arrays = {
        "x": np.asarray(x), "xT": np.asarray(x).transpose(0, 2, 1), "adj": np.asarray(adj),
        "wqT": grouped(L0_gnn_Wq), "wkT": grouped(L0_gnn_Wk), "wvT": np.asarray(L0_gnn_Wv).T,
        "bv": np.asarray(L0_gnn_bv), "woT": np.asarray(L0_gnn_Wo).T, "bo": np.asarray(L0_gnn_bo),
    }
    arrays = {k: np.ascontiguousarray(a) for k, a in arrays.items()}
    nc = bacc.Bacc("TRN2", target_bir_lowering=False, num_devices=1)
    args = [nc.dram_tensor(f"in_{k}", arrays[k].shape, mybir.dt.from_np(arrays[k].dtype), kind="ExternalInput").ap()
            for k in _INS]
    y = nc.dram_tensor("out_y", (B, N, D), F32, kind="ExternalOutput").ap()
    build(nc, *args, y)
    r = run_bass_kernel_spmd(nc, [{f"in_{k}": arrays[k] for k in _INS}], core_ids=[0])
    return r.results[0]["out_y"]
```

```python
import concourse.bass as bass
from concourse import mybir

F32 = mybir.dt.float32
F32R = mybir.dt.float32r
BF16 = mybir.dt.bfloat16
I32 = mybir.dt.int32
ALU = mybir.AluOpType
ACT = mybir.ActivationFunctionType
AX = mybir.AxisListType

B, N, D = 32, 256, 384
H, HD = 12, 32
P = 128
KC = D // P
NT = N // P
JH = P // HD
SCALE = D ** -0.5
EPS = 1e-5
BIG = 3.0e38

S_BANKS, P_RING, PT_RING = 2, 4, 6
WARM_START, WARM_STACKS, WARM_END = 24, 8, 28
DMA = 16
STACK_DMAS, STACK_DMAS_0 = 6, 12
HALF = H // 2

PROJECT, FINISH = ("K01", "K2Q0", "Q12", "V0", "V1"), ("sumT", "R01", "R2", "Y0", "Y1")
BANK = {"K01": 0, "sumT": 2, "K2Q0": 1, "R01": 2, "R2": 1, "Q12": 0, "V0": 2, "V1": 1, "Y0": 0, "Y1": 2}
PLAN = [
    [("K01", 0, 4)],
    [("K01", 4, 6), ("K2Q0", 0, 1)],
    [("K2Q0", 1, 3)],
    [("K2Q0", 3, 5), ("sumT", 0, 1), ("K2Q0", 5, 6)],
    [("Q12", 0, 3)],
    [("R01", 0, 1), ("Q12", 3, 5), ("R2", 0, 1), ("Q12", 5, 6)],
    [("V0", 0, 1)],
    [("V0", 1, 3), ("V1", 0, 1)],
    [("V1", 1, 3)],
    [("Y0", 0, 3)],
    [],
    [("Y1", 0, 3)],
]

EARLY_0 = [("K01", 0, 6), ("K2Q0", 0, 2)]
PLAN_0 = [
    [("K2Q0", 2, 4)],
    [("K2Q0", 4, 6)],
    [("Q12", 0, 2)],
    [("Q12", 2, 4)],
    [("Q12", 4, 6)],
    [("V0", 0, 1)],
    [("V0", 1, 3)],
    [("V1", 0, 1)],
    [("V1", 1, 3)],
    [],
    [],
    [],
]


class Step:

    def __init__(self, i, c):
        self.i, self.c, self.n, self.p = i, c, 2 * i + c, c % 2
        looped = not isinstance(i, int)
        self.attend = looped or 0 <= c < B
        self.finish = looped or 1 <= c <= B
        self.project = looped or -1 <= c <= B - 2
        self.looped = looped
        self.first = not looped and c == 0
        self.last = not looped and c == B

    def count(self, per_step, extra=0):
        return self.i * (2 * per_step) + (self.c * per_step + extra)

    def units(self):
        return [u for u in BANK if (u in PROJECT and self.project) or (u in FINISH and self.finish)]

    def units_before(self, name=None):
        k = 0 if name is None else self.units().index(name)
        if not self.looped and not 1 <= self.c < B:
            return {-1: 0, 0: len(PROJECT), B: len(BANK) * (B - 1) + len(BANK) // 2}[self.c] + k
        return self.count(len(BANK), k)

    def before(self):
        return Step(self.i, self.c - 1)

    def last_user(self, name):
        order = self.units()
        mine = [u for u in order[:order.index(name)] if BANK[u] == BANK[name]]
        if mine:
            return self.units_before(mine[-1]) + 1
        t = self.before()
        while t.looped or t.c >= -1:
            users = [u for u in t.units() if BANK[u] == BANK[name]]
            if users:
                return t.units_before(users[-1]) + 1
            t = t.before()
        return None

    def head(self, h):
        return (self, h) if h >= 0 else (self.before(), h + H)


def plan(t, h):
    if t.c == B - 1 and h in (9, 11):
        return PLAN[9] + PLAN[11] if h == 11 else []
    if t.first:
        return PLAN_0[h]
    return [w for w in PLAN[h] if w[0] in t.units()]


def kq_unit(t, h):
    at = 1 if t.first else 2
    return {at: "K01", at + 2: "K2Q0", at + 4: "Q12"}.get(h) if t.project else None


def on_dve(h):
    return h % 3 == 1


def dve_heads(t, h):
    return t.count(H // 3, (h + 2) // 3)


def act_heads(t, h):
    return t.count(H - H // 3, h + 1 - (h + 2) // 3)


def steps(eng, body):
    for c in range(-1, 3):
        body(Step(0, c))
    with eng.Fori(1, (B - 4) // 2) as i:
        body(Step(i, 1))
        body(Step(i, 2))
    for c in range(B - 3, B + 2):
        body(Step(0, c))


def build(nc, x, xT, adj, wqT, wkT, wvT, bv, woT, bo, out):
    def sb(name, shape, dt=F32):
        return nc.alloc_sbuf_tensor(name, shape, dt)

    ident = sb("ident", [P, P])
    ones = sb("ones", [P, P], BF16)
    sel_f = sb("sel_f", [HD + H, D])
    sel = sb("sel", [HD + H, D], F32R)
    halfs = sb("halfs", [P, NT])
    w_hi = sb("w_hi", [P, 4, KC, D], F32R)
    w_lo = sb("w_lo", [P, 4, KC, D], F32R)
    bv_all = sb("bv_all", [P, D])
    bo_all = sb("bo_all", [P, D])
    xt = [sb(f"xt{p}", [P, KC, N]) for p in range(2)]
    xt_hi = [sb(f"xt_hi{p}", [P, KC, N], F32R) for p in range(2)]
    xt_lo = [sb(f"xt_lo{p}", [P, KC, N], F32R) for p in range(2)]
    xr = [sb(f"xr{p}", [P, NT, D]) for p in range(2)]
    bias = [sb(f"bias{p}", [P, NT, N]) for p in range(2)]
    kq_hi = sb("kq_hi", [P, 2 * KC, N], F32R)
    kq_lo = sb("kq_lo", [P, 2 * KC, N], F32R)
    k_stack = [sb(f"k_stack{p}", [3 * HD, H, N], F32R) for p in range(2)]
    q_stack = [sb(f"q_stack{p}", [3 * HD, H, N], F32R) for p in range(2)]
    v = [sb(f"v{p}", [P, NT, D]) for p in range(2)]
    neg = sb("neg", [P, H, NT, N])
    w_f = (neg[:, 0:4 * KC * D // (NT * N)].rearrange("p h c n -> p (h c n)")
           .rearrange("p (w k d) -> p w k d", w=4, k=KC))
    negmax = [sb(f"negmax{p}", [P, NT, H]) for p in range(2)]
    sums = [sb(f"sums{p}", [P, NT, H]) for p in range(2)]
    prob = sb("prob", [P, P_RING, NT, N])
    probT = sb("probT", [P, PT_RING, NT, N])
    zero_max = [sb(f"zero_max{g}", [P, NT, HALF], BF16) for g in range(2)]
    zero_flag = sb("zero_flag", [1, 1], I32)
    most = sb("most", [P, NT, H])
    keep = sb("keep", [P, NT, H])
    recip = sb("recip", [P, NT, H])
    inv = sb("inv", [P, NT, H])
    inv_t = sb("inv_t", [HD + H, N], F32R)
    o_raw = [sb(f"o_raw{p}", [P, KC, N]) for p in range(2)]
    o_n = sb("o_n", [P, KC, N])
    o_hi = sb("o_hi", [P, KC, N], F32R)
    o_lo = sb("o_lo", [P, KC, N], F32R)
    y = sb("y", [P, NT, D])
    stats = sb("stats", [P, NT, 6])
    meanvar = sb("meanvar", [P, NT, 2])
    var_eps = sb("var_eps", [P, NT])
    rstd = sb("rstd", [P, NT])
    y_out = sb("y_out", [P, NT, D])

    s_bank = [nc.alloc_psum_tensor(f"s_bank{k}", [P, NT, N], F32) for k in range(S_BANKS)]
    t_bank = [nc.alloc_psum_tensor(f"t_bank{k}", [P, NT, N], F32) for k in range(2)]
    o_bank = nc.alloc_psum_tensor("o_bank", [P, NT * N], F32)
    shared = [nc.alloc_psum_tensor(f"shared{k}", [P, NT * N], F32) for k in range(3)]
    flags_at = o_bank[:, N:N + NT * HALF]

    W_Q, W_K, W_V, W_O = range(4)
    W_SPLIT = {W_Q: KC + 1, W_V: KC + 2, W_O: KC + 3}
    sem = nc.alloc_semaphore
    const_ready = sem("const_ready")
    wk_loaded = [sem(f"wk_loaded{k}") for k in range(KC)]
    w_loaded = {w: sem(f"w_loaded_{name}") for w, name in ((W_Q, "q"), (W_V, "v"), (W_O, "o"))}
    b_loaded = sem("b_loaded")
    w_hi_ready = sem("w_hi_ready")
    w_ready = sem("w_ready")
    xt_loaded = [sem(f"xt_loaded{p}") for p in range(2)]
    xr_loaded = [sem(f"xr_loaded{p}") for p in range(2)]
    bias_loaded = [sem(f"bias_loaded{p}") for p in range(2)]
    xt_hi_ready = sem("xt_hi_ready")
    xt_ready = sem("xt_ready")
    xr_ready = sem("xr_ready")
    kq_hi_ready = sem("kq_hi_ready")
    stacked = sem("stacked")
    scored = sem("scored")
    neg_ready = sem("neg_ready")
    prob_ready = sem("prob_ready")
    transposed = sem("transposed")
    probT_dve = sem("probT_dve")
    probT_act = sem("probT_act")
    pv_done = sem("pv_done")
    o_saved = sem("o_saved")
    unit_done = sem("unit_done")
    unit_free = sem("unit_free")
    zero_found = sem("zero_found")
    flag_done = sem("flag_done")
    flag_read = sem("flag_read")
    keep_set = sem("keep_set")
    recip_ready = sem("recip_ready")
    inv_hi_ready = sem("inv_hi_ready")
    bn_ready = sem("bn_ready")
    inv_ready = sem("inv_ready")
    o_hi_ready = sem("o_hi_ready")
    o_ready = sem("o_ready")
    stats_ready = sem("stats_ready")
    var_ready = sem("var_ready")
    rstd_ready = sem("rstd_ready")
    y_ready = sem("y_ready")
    stored = sem("stored")
    passed = sem("passed")

    KQ = {"K01": [(W_K, 0), (W_K, 1)], "K2Q0": [(W_K, 2), (W_Q, 0)], "Q12": [(W_Q, 1), (W_Q, 2)]}
    KQ_AT = {"K01": 0, "K2Q0": 2, "Q12": 4}
    STACKED = (("hi", "hi", "lo"), ("hi", "lo", "hi"))

    def apart(eng):
        eng.sem_inc(passed, 1)

    def split_o_lo(eng, t):
        eng.wait_ge(unit_free, t.units_before("R2") + 1)
        if t.looped or t.c >= 2:
            eng.wait_ge(unit_done, t.units_before())
        eng.wait_ge(o_hi_ready, t.count(1))
        eng.tensor_tensor(o_lo[:], o_n[:], o_hi[:].bitcast(F32), ALU.subtract).then_inc(o_ready, 1)

    with nc.Block() as block:

        @block.sync
        def _(sp):
            def load_xt(t, k):
                sp.dma_start(xt[(t.c + k) % 2][:], xT[t.n + k].rearrange("(c p) n -> p c n", p=P)
                             ).then_inc(xt_loaded[(t.c + k) % 2], DMA)

            load_xt(Step(0, 0), 0)
            for k in range(KC):
                sp.dma_start(w_f[:, W_K, k], wkT[P * k:P * (k + 1), :]).then_inc(wk_loaded[k], DMA)
            for w, src in ((W_Q, wqT), (W_V, wvT), (W_O, woT)):
                sp.dma_start(w_f[:, w], src.rearrange("(c p) n -> p c n", p=P)).then_inc(w_loaded[w], DMA)
            load_xt(Step(0, 0), 1)
            for dst, src in ((bv_all, bv), (bo_all, bo)):
                sp.dma_start(dst[:], src.rearrange("(a n) -> a n", a=1).to_broadcast([P, D])
                             ).then_inc(b_loaded, DMA)

            def stack(t, k, rows, a=0, b=KC):
                dst = (k_stack, q_stack)[k][(t.c + 1) % 2]
                for r in rows:
                    part = (kq_hi, kq_lo)[STACKED[k][r] == "lo"]
                    sp.dma_start(dst[HD * r:HD * (r + 1)].rearrange("d (j c) n -> d j c n", j=JH)[:, :, a:b]
                                 .bitcast(F32), part[:, KC * k + a:KC * k + b, :].bitcast(F32)
                                 ).then_inc(stacked, DMA)

            def stack_first(t):
                for name in KQ:
                    ranges = {"K01": [(0, 0, 2)], "K2Q0": [(0, 2, 3), (1, 0, 1)], "Q12": [(1, 1, 3)]}[name]
                    sp.wait_ge(kq_hi_ready, KQ_AT[name] // 2 + 1)
                    for k, a, b in ranges:
                        stack(t, k, [r for r in range(3) if STACKED[k][r] == "hi"], a, b)
                    sp.wait_ge(unit_free, t.units_before(name) + 1)
                    for k, a, b in ranges:
                        stack(t, k, [STACKED[k].index("lo")], a, b)

            def step(t):
                if t.looped or 0 <= t.c <= B - 4:
                    sp.wait_ge(xt_ready, t.count(1, 2))
                    load_xt(t, 3)
                if t.project:
                    q = (t.c + 1) % 2
                    if t.looped or t.c >= 1:
                        sp.wait_ge(neg_ready, t.count(H * NT))
                    sp.dma_start(bias[q][:], adj[t.n + 1].rearrange("(c p) m -> p c m", p=P)
                                 ).then_inc(bias_loaded[q], DMA)
                if t.attend:
                    if t.looped or t.c >= 2:
                        sp.wait_ge(unit_free, t.units_before())
                    sp.dma_start(xr[t.p][:], x[t.n].rearrange("(c p) d -> p c d", p=P)
                                 ).then_inc(xr_loaded[t.p], DMA)
                if t.c == -1:
                    stack_first(t)
                    sp.wait_ge(xt_ready, 1)
                    load_xt(t, 3)
                elif t.project:
                    if t.looped or t.c >= 1:
                        sp.wait_ge(scored, t.count(H))
                        apart(sp)
                    sp.wait_ge(kq_hi_ready, t.count(3, 3 + 2))
                    apart(sp)
                    sp.wait_ge(unit_free, t.units_before("K2Q0") + 1)
                    stack(t, 0, range(3))
                    sp.wait_ge(kq_hi_ready, t.count(3, 3 + 3))
                    apart(sp)
                    sp.wait_ge(unit_free, t.units_before("Q12") + 1)
                    stack(t, 1, range(3))
                if t.before().finish:
                    sp.wait_ge(y_ready, t.count(NT, -NT))
                    sp.dma_start(out[t.n - 2].rearrange("(c p) d -> p c d", p=P), y_out[:]
                                 ).then_inc(stored, DMA)

            steps(sp, step)
            sp.wait_ge(stored, DMA * B)

        @block.gpsimd
        def _(pool):
            nc.gpsimd.memset(ones[:], 1.0).then_inc(const_ready, 1)
            nc.gpsimd.memset(ident[:], 0.0).then_inc(const_ready, 1)
            nc.gpsimd.memset(sel_f[:], 1.0).then_inc(const_ready, 1)
            nc.gpsimd.memset(halfs[:], -0.5).then_inc(const_ready, 1)
            nc.gpsimd.memset(inv_t[:].bitcast(F32), 0.0).then_inc(const_ready, 1)
            pool.wait_ge(const_ready, 5)
            nc.gpsimd.affine_select(out=ident[:], in_=ident[:], compare_op=ALU.not_equal, fill=1.0,
                                    base=0, pattern=[[-1, P]], channel_multiplier=1).then_inc(const_ready, 1)
            for k, (at, n) in enumerate(((0, HD), (HD, H))):
                rows = sel_f[at:at + n, :]
                pool.wait_ge(const_ready, 6 + 2 * k)
                nc.gpsimd.affine_select(out=rows, in_=rows, compare_op=ALU.is_ge, fill=0.0,
                                        base=0, pattern=[[1, D]], channel_multiplier=-HD).then_inc(const_ready, 1)
                pool.wait_ge(const_ready, 7 + 2 * k)
                nc.gpsimd.affine_select(out=rows, in_=rows, compare_op=ALU.is_ge, fill=0.0,
                                        base=HD - 1, pattern=[[-1, D]], channel_multiplier=HD).then_inc(const_ready, 1)
            pool.wait_ge(const_ready, 10)
            nc.gpsimd.tensor_copy(sel[:], sel_f[:]).then_inc(const_ready, 1)

            def split_xt(t, k):
                q = (t.c + k) % 2
                pool.wait_ge(xt_loaded[q], DMA * ((t.c + k) // 2 + 1) + t.i * DMA)
                apart(pool)
                nc.gpsimd.tensor_copy(xt_hi[q][:], xt[q][:]).then_inc(xt_hi_ready, 1)
                pool.wait_ge(xt_hi_ready, t.count(1, k + 1))
                nc.gpsimd.tensor_tensor(xt_lo[q][:], xt[q][:], xt_hi[q][:].bitcast(F32), ALU.subtract
                                        ).then_inc(xt_ready, 1)

            def step(t):
                if t.c == -1:
                    pool.wait_ge(xt_ready, 1)
                if t.looped or t.c <= B - 3:
                    if t.looped or t.c >= 0:
                        pool.wait_ge(unit_done, t.units_before())
                    split_xt(t, 2)
                if t.before().finish:
                    pool.wait_ge(stats_ready, t.count(NT, -NT))
                    apart(pool)
                    nc.gpsimd.tensor_scalar(var_eps[:], meanvar[:, :, 1], EPS, None, ALU.add
                                            ).then_inc(var_ready, 1)
                    pool.wait_ge(var_ready, t.count(1, -1))
                    nc.gpsimd.tensor_tensor(rstd[:], var_eps[:], halfs[:], ALU.pow).then_inc(rstd_ready, 1)
                if t.attend:
                    pool.wait_ge(b_loaded, 2 * DMA)
                    pool.wait_ge(xr_loaded[t.p], DMA * (t.c // 2 + 1) + t.i * DMA)
                    nc.gpsimd.tensor_tensor(xr[t.p][:], xr[t.p][:], bo_all[:].unsqueeze(1).to_broadcast([P, NT, D]),
                                            ALU.add).then_inc(xr_ready, 1)
                if t.c == B - 1:
                    pool.wait_ge(unit_free, t.units_before("R2") + 1)
                    pool.wait_ge(unit_done, t.units_before())
                    nc.gpsimd.tensor_copy(o_hi[:], o_n[:]).then_inc(o_hi_ready, 1)
                if t.finish and not t.last:
                    split_o_lo(pool, t)

            steps(pool, step)

        @block.scalar
        def _(act):
            for k in range(KC):
                act.wait_ge(wk_loaded[k], DMA)
                nc.scalar.activation(w_hi[:, W_K, k], w_f[:, W_K, k], ACT.Copy).then_inc(w_hi_ready, 1)

            def w_hi_part(w):
                act.wait_ge(w_loaded[w], DMA)
                nc.scalar.activation(w_hi[:, w], w_f[:, w], ACT.Copy, scale=SCALE if w == W_Q else 1.0
                                     ).then_inc(w_hi_ready, 1)

            w_hi_part(W_Q)

            def kq_hi_part(t, name):
                act.wait_ge(unit_done, t.units_before(name) + 1)
                if name == "K01" and (t.looped or t.c >= 0):
                    act.wait_ge(stacked, t.count(STACK_DMAS * DMA, STACK_DMAS_0 * DMA))
                a = KQ_AT[name]
                nc.scalar.activation(kq_hi[:, a:a + 2, :], shared[BANK[name]][:].rearrange("p (a n) -> p a n", a=2),
                                     ACT.Copy).then_inc(kq_hi_ready, 1)

            def copy_probT(t, h):
                g = t.count(H, h)
                act.wait_ge(transposed, g + 1)
                if t.looped or g >= PT_RING:
                    act.wait_ge(pv_done, t.count(KC, (h - PT_RING) // JH + 1))
                nc.scalar.activation(probT[:, h % PT_RING], t_bank[h % 2][:], ACT.Copy).then_inc(probT_act, 1)

            def exps(t, h):
                g = t.count(H, h)
                if t.looped or g >= P_RING:
                    act.wait_ge(transposed, g - P_RING + 1)
                for c in range(NT):
                    act.wait_ge(neg_ready, t.count(H * NT, NT * h + c + 1))
                    if h == 0 and (t.looped or t.c >= 2):
                        act.wait_ge(inv_ready, t.count(1, -1))
                    nc.scalar.activation(prob[:, h % P_RING, c], neg[:, h, c], ACT.Exp, scale=-1.0,
                                         bias=negmax[t.p][:, c, h:h + 1], accum_out=sums[t.p][:, c, h:h + 1]
                                         ).then_inc(prob_ready, 1)

            def split_o(t):
                act.wait_ge(unit_free, t.units_before("R2") + 1)
                if t.looped or t.c >= 2:
                    act.wait_ge(unit_done, t.units_before())
                nc.scalar.activation(o_hi[:], o_n[:], ACT.Copy).then_inc(o_hi_ready, 1)

            def save_o(t, c):
                act.wait_ge(pv_done, t.count(KC, c + 1))
                if c == 0:
                    act.wait_ge(flag_done, t.count(2, 1))
                if c == 0 and (t.looped or t.c >= 2):
                    act.wait_ge(unit_free, t.units_before())
                nc.scalar.activation(o_raw[t.p][:, c, :], o_bank[:, 0:N], ACT.Copy).then_inc(o_saved, 1)

            def step(t):
                for h in range(H):
                    if t.c == -1 and h in (3, 7):
                        w_hi_part({3: W_V, 7: W_O}[h])
                    if kq_unit(t, h):
                        kq_hi_part(t, kq_unit(t, h))
                    if (t.attend and h >= 2) or (t.finish and h < 2):
                        s, hh = t.head(h - 2)
                        if not on_dve(hh):
                            copy_probT(s, hh)
                    if t.attend:
                        exps(t, h)
                    if h == 3 and t.finish:
                        save_o(t.head(-1)[0], 2)
                    if h in (7, 11) and t.attend:
                        save_o(t, h // 4 - 1)
                    if h == 6 and t.finish and t.c != B - 1:
                        split_o(t)

            steps(act, step)

        @block.tensor
        def _(pe):
            def product(ps, w_pair, m_pair, k):
                for e, (a, b) in enumerate(((0, 0), (0, 1), (1, 0))):
                    last = nc.tensor.matmul(ps, w_pair[a](k), m_pair[b](k),
                                            start=(k == 0 and e == 0), stop=(k == KC - 1 and e == 2))
                return last

            def unit(t, name, first, end):
                bank = shared[BANK[name]]
                q = (t.c + 1) % 2
                if first == 0:
                    used = t.last_user(name)
                    if used is not None:
                        pe.wait_ge(unit_free, used)
                    if name == "K01":
                        pe.wait_ge(xt_ready, t.count(1, 2))
                    if t.c == 1 and not t.looped and name == "Y0":
                        pe.wait_ge(w_ready, W_SPLIT[W_O])
                    if name == "sumT":
                        pe.wait_ge(inv_ready, t.count(1))
                    if name in ("R01", "R2"):
                        pe.wait_ge(unit_free, t.units_before("sumT") + 1)
                    if name == "Y0":
                        pe.wait_ge(o_ready, t.count(1))
                for piece in range(first, end):
                    k = piece % KC
                    if t.c == -1:
                        splits = {"K01": min(piece + 1, KC), "K2Q0": KC if piece < KC else W_SPLIT[W_Q],
                                  "Q12": W_SPLIT[W_Q], "V0": W_SPLIT[W_V], "V1": W_SPLIT[W_V]}[name]
                        pe.wait_ge(w_ready, splits)
                    if name in KQ:
                        part = piece // KC
                        w, c = KQ[name][part]
                        last = product(bank[:, N * part:N * (part + 1)],
                                       [lambda k, a=a: a[:, w, k, P * c:P * (c + 1)] for a in (w_hi, w_lo)],
                                       [lambda k, a=a: a[q][:, k, :] for a in (xt_hi, xt_lo)], k)
                        ends = piece == 2 * KC - 1
                    elif name == "sumT":
                        for c in range(NT):
                            last = nc.tensor.matmul(bank[0:H, P * c:P * (c + 1)], inv[:, c, :], ident[:],
                                                    start=True, stop=True)
                        ends = True
                    elif name in ("R01", "R2"):
                        for c in ((0, 1) if name == "R01" else (2,)):
                            ps = bank[:, N * (c % 2):N * (c % 2 + 1)]
                            last = nc.tensor.matmul(ps, sel[:, P * c:P * (c + 1)], inv_t[:], start=True, stop=True)
                        ends = True
                    else:
                        c = int(name[1])
                        src = [lambda k, a=a: a[:, k, P * c:P * (c + 1)]
                               for a in ((xt_hi[q], xt_lo[q]) if name[0] == "V" else (o_hi, o_lo))]
                        w = W_V if name[0] == "V" else W_O
                        last = product(bank[:, 0:D], src, [lambda k, a=a: a[:, w, k, :] for a in (w_hi, w_lo)], k)
                        ends = k == KC - 1
                if ends:
                    last.then_inc(unit_done, 1)

            def flag(t, g):
                pe.wait_ge(zero_found, t.count(2, g + 1))
                if g == 1:
                    pe.wait_ge(o_saved, t.count(KC, 2))
                nc.tensor.matmul(flags_at, ones[:], zero_max[g][:], start=True, stop=True).then_inc(flag_done, 1)

            def scores(t, h):
                if h == 0:
                    pe.wait_ge(stacked, t.count(STACK_DMAS * DMA, STACK_DMAS_0 * DMA))
                if t.looped or t.count(H, h) >= S_BANKS:
                    pe.wait_ge(neg_ready, t.count(H * NT, NT * (h - S_BANKS + 1)))
                for c in range(NT):
                    last = nc.tensor.matmul(s_bank[h % S_BANKS][:, c, :], q_stack[t.p][:, h, P * c:P * (c + 1)],
                                            k_stack[t.p][:, h, :], start=True, stop=True)
                last.then_inc(scored, 1)

            def transposes(t, h):
                pe.wait_ge(prob_ready, t.count(H * NT, NT * (h + 1)))
                if t.looped or t.count(H, h) >= 2:
                    s, hh = t.head(h - 2)
                    if on_dve(hh):
                        pe.wait_ge(probT_dve, dve_heads(s, hh))
                    else:
                        pe.wait_ge(probT_act, act_heads(s, hh))
                for m in range(NT):
                    for c in range(NT):
                        last = nc.tensor.transpose(t_bank[h % 2][:, m, P * c:P * (c + 1)],
                                                   prob[:, h % P_RING, c, P * m:P * (m + 1)], ident[:])
                last.then_inc(transposed, 1)

            def weigh(t, c):
                h = JH * c + JH - 1
                pe.wait_ge(probT_dve, dve_heads(t, h))
                pe.wait_ge(probT_act, act_heads(t, h))
                if c == 0:
                    pe.wait_ge(unit_free, t.units_before())
                if t.looped or t.count(KC, c) >= 1:
                    pe.wait_ge(o_saved, t.count(KC, c))
                if t.looped or t.count(2, c) >= 1:
                    pe.wait_ge(flag_read, t.count(2, c))
                for m in range(NT):
                    for j in range(JH):
                        h = JH * c + j
                        last = nc.tensor.matmul(o_bank[HD * j:HD * (j + 1), 0:N], v[t.p][:, m, HD * h:HD * (h + 1)],
                                                probT[:, h % PT_RING, m, :], start=(m == 0), stop=(m == NT - 1))
                last.then_inc(pv_done, 1)

            def keep_warm(products):
                for _ in range(products):
                    nc.tensor.matmul(s_bank[0][:, 0, :], ones[:], ones[:].unsqueeze(1).to_broadcast([P, NT, P]),
                                     start=True, stop=True)

            pe.wait_ge(const_ready, 1)
            keep_warm(WARM_START)
            pe.wait_ge(const_ready, 11)

            def step(t):
                if t.first:
                    for name, first, end in EARLY_0:
                        unit(t, name, first, end)
                    keep_warm(WARM_STACKS)
                for h in range(H):
                    if t.attend:
                        scores(t, h)
                    if (t.attend and h >= 2) or (t.finish and h < 2):
                        transposes(*t.head(h - 2))
                    if h in (6, 10) and t.attend:
                        weigh(t, h // 4 - 1)
                    if h == 6 and t.attend:
                        flag(t, 0)
                    for name, first, end in plan(t, h):
                        unit(t, name, first, end)
                    if h == 2 and t.finish:
                        weigh(t.before(), 2)
                    if h == 0 and t.finish:
                        flag(t.before(), 1)
                    if h == 5 and t.last:
                        pe.wait_ge(neg_ready, t.count(H * NT))
                        keep_warm(WARM_END)

            steps(pe, step)

        @block.vector
        def _(dve):
            any_zero = dve.alloc_register("any_zero")
            dve.wait_ge(xt_loaded[0], DMA)
            nc.vector.tensor_copy(xt_hi[0][:], xt[0][:]).then_inc(xt_hi_ready, 1)
            dve.wait_ge(xt_hi_ready, 1)
            nc.vector.tensor_tensor(xt_lo[0][:], xt[0][:], xt_hi[0][:].bitcast(F32), ALU.subtract
                                    ).then_inc(xt_ready, 1)
            for k in range(KC):
                dve.wait_ge(w_hi_ready, k + 1)
                nc.vector.tensor_tensor(w_lo[:, W_K, k], w_f[:, W_K, k], w_hi[:, W_K, k].bitcast(F32), ALU.subtract
                                        ).then_inc(w_ready, 1)

            def w_lo_part(w):
                dve.wait_ge(w_hi_ready, W_SPLIT[w])
                nc.vector.scalar_tensor_tensor(out=w_lo[:, w], in0=w_f[:, w], scalar=SCALE if w == W_Q else 1.0,
                                               in1=w_hi[:, w].bitcast(F32), op0=ALU.mult, op1=ALU.subtract
                                               ).then_inc(w_ready, 1)

            w_lo_part(W_Q)

            def add_bias(t, h):
                dve.wait_ge(scored, t.count(H, h + 1))
                if h == 0 and t.first:
                    dve.wait_ge(w_ready, W_SPLIT[W_O])
                if h == 0:
                    dve.wait_ge(bias_loaded[t.p], DMA * (t.c // 2 + 1) + t.i * DMA)
                if t.looped or t.c >= 1:
                    dve.wait_ge(prob_ready, t.count(H * NT, NT * (h + 1) - H * NT))
                apart(dve)
                for c in range(NT):
                    nc.vector.tensor_tensor_reduce(out=neg[:, h, c], in0=s_bank[h % S_BANKS][:, c, :],
                                                   in1=bias[t.p][:, c, :], scale=-1.0, scalar=BIG,
                                                   op0=ALU.add, op1=ALU.min,
                                                   accum_out=negmax[t.p][:, c, h:h + 1]).then_inc(neg_ready, 1)

            def copy_probT(t, h):
                g = t.count(H, h)
                dve.wait_ge(transposed, g + 1)
                if t.looped or g >= PT_RING:
                    dve.wait_ge(pv_done, t.count(KC, (h - PT_RING) // JH + 1))
                nc.vector.tensor_copy(probT[:, h % PT_RING], t_bank[h % 2][:]).then_inc(probT_dve, 1)

            def kq_lo_part(t, name):
                a = KQ_AT[name]
                dve.wait_ge(kq_hi_ready, t.count(3, 3 + a // 2 + 1))
                nc.vector.tensor_tensor(kq_lo[:, a:a + 2, :], shared[BANK[name]][:].rearrange("p (a n) -> p a n", a=2),
                                        kq_hi[:, a:a + 2, :].bitcast(F32), ALU.subtract).then_inc(unit_free, 1)

            def save_v(t, c):
                name = f"V{c}"
                dve.wait_ge(unit_done, t.units_before(name) + 1)
                if c == 0:
                    dve.wait_ge(b_loaded, 2 * DMA)
                    if t.looped or t.c >= 1:
                        dve.wait_ge(pv_done, t.count(KC))
                nc.vector.tensor_tensor(v[(t.c + 1) % 2][:, c, :], shared[BANK[name]][:, 0:D], bv_all[:], ALU.add
                                        ).then_inc(unit_free, 1)

            def find_zero(t, g):
                dve.wait_ge(neg_ready, t.count(H * NT, NT * HALF * (g + 1)))
                if t.looped or t.c >= 1:
                    dve.wait_ge(flag_done, t.count(2, g - 1))
                heads = slice(HALF * g, HALF * (g + 1))
                nc.vector.tensor_scalar(zero_max[g][:], negmax[t.p][:, :, heads], 0.0, None, ALU.is_equal
                                        ).then_inc(zero_found, 1)

            def read_flag(t, g):
                if g == 0:
                    if t.looped or t.c >= 1:
                        dve.wait_ge(inv_ready, t.count(1))
                    nc.vector.memset(keep[:], 1.0).then_inc(keep_set, 1)
                dve.wait_ge(flag_done, t.count(2, g + 1))
                dve.wait_ge(o_saved, t.count(KC, g + 1))
                nc.vector.tensor_reduce(zero_flag[:], flags_at[0:1, :], AX.X, ALU.max).then_inc(flag_read, 1)

            def mask(t, g):
                heads = slice(HALF * g, HALF * (g + 1))
                dve.wait_ge(flag_read, t.count(2, g + 1))
                dve.wait_ge(zero_found, t.count(2, g + 1))
                dve.wait_ge(keep_set, t.count(1, 1))
                apart(dve)
                dve.reg_load(any_zero, zero_flag[0:1, 0:1])
                with dve.If_ne(any_zero, 0):
                    nc.vector.tensor_reduce(most[:, :, heads].rearrange("p c h -> p h c"), neg[:, heads], AX.X, ALU.max)
                    dve.drain()
                    nc.vector.scalar_tensor_tensor(out=keep[:, :, heads], in0=most[:, :, heads], scalar=0.0,
                                                   in1=zero_max[g][:], op0=ALU.is_equal, op1=ALU.mult)
                    dve.drain()
                    nc.vector.tensor_scalar(keep[:, :, heads], keep[:, :, heads], -1.0, 1.0, ALU.mult, ALU.add)
                    dve.drain()

            def invert(t):
                p = (t.c + 1) % 2
                dve.wait_ge(prob_ready, t.count(H * NT))
                nc.vector.reciprocal(recip[:], sums[p][:]).then_inc(recip_ready, 1)
                if t.looped or t.c >= 2:
                    dve.wait_ge(unit_done, t.before().units_before("sumT") + 1)
                dve.wait_ge(recip_ready, t.count(1))
                nc.vector.tensor_tensor(inv[:], recip[:], keep[:], ALU.mult).then_inc(inv_ready, 1)

            def split_inv(t):
                bank = shared[BANK["sumT"]]
                dve.wait_ge(unit_done, t.units_before("sumT") + 1)
                dve.wait_ge(const_ready, 11)
                nc.vector.tensor_copy(inv_t[0:H, :], bank[0:H, 0:N]).then_inc(inv_hi_ready, 1)
                dve.wait_ge(inv_hi_ready, t.count(1))
                nc.vector.tensor_tensor(inv_t[HD:HD + H, :], bank[0:H, 0:N], inv_t[0:H, :].bitcast(F32), ALU.subtract
                                        ).then_inc(unit_free, 1)

            def divide(t):
                p = (t.c + 1) % 2
                dve.wait_ge(o_saved, t.count(KC))
                if t.looped or t.c >= 2:
                    dve.wait_ge(o_ready, t.count(1, -1))
                for name, a, b in (("R01", 0, 2), ("R2", 2, 3)):
                    dve.wait_ge(unit_done, t.units_before(name) + 1)
                    nc.vector.tensor_tensor(o_n[:, a:b, :], o_raw[p][:, a:b, :],
                                            shared[BANK[name]][:, 0:N * (b - a)].rearrange("p (a n) -> p a n", n=N),
                                            ALU.mult).then_inc(unit_free, 1)

            def residual(t, c):
                p = (t.c + 1) % 2
                name = f"Y{c}"
                dve.wait_ge(unit_done, t.units_before(name) + 1)
                dve.wait_ge(xr_ready, t.count(1))
                if c == 0 and t.before().finish:
                    dve.wait_ge(y_ready, t.count(NT, -NT))
                nc.vector.tensor_tensor(y[:, c, :], shared[BANK[name]][:, 0:D], xr[p][:, c, :], ALU.add
                                        ).then_inc(unit_free, 1)
                dve.wait_ge(unit_free, t.units_before(name) + 1)
                nc.vector.bn_stats(stats[:, c, :], y[:, c, :]).then_inc(bn_ready, 1)
                dve.wait_ge(bn_ready, t.count(NT, c + 1 - NT))
                apart(dve)
                nc.vector.bn_aggr(meanvar[:, c, :], stats[:, c, :]).then_inc(stats_ready, 1)

            def normalise(t):
                dve.wait_ge(rstd_ready, t.count(1))
                if t.looped or t.c >= 2:
                    dve.wait_ge(stored, t.count(DMA, -DMA))
                for c in range(NT):
                    nc.vector.tensor_scalar(y_out[:, c, :], y[:, c, :], meanvar[:, c, 0:1], rstd[:, c:c + 1],
                                            ALU.subtract, ALU.mult).then_inc(y_ready, 1)

            def step(t):
                for h in range(H):
                    if t.attend:
                        add_bias(t, h)
                    if (t.attend and h >= 2) or (t.finish and h < 2):
                        s, hh = t.head(h - 2)
                        if on_dve(hh):
                            copy_probT(s, hh)
                    if h == 0 and t.before().finish and not t.last:
                        residual(t.before(), 1)
                    if h == 0 and t.finish:
                        read_flag(t.before(), 1)
                    if h == 1 and t.finish:
                        mask(t.before(), 1)
                    if h == 2 and t.finish:
                        invert(t)
                        if t.last:
                            residual(t.before(), 1)
                    if t.c == -1 and h in (3, 7):
                        w_lo_part({3: W_V, 7: W_O}[h])
                    if kq_unit(t, h):
                        kq_lo_part(t, kq_unit(t, h))
                    if h == 3 and t.finish:
                        split_inv(t)
                    if h == 5 and t.finish:
                        divide(t)
                        if t.last:
                            split_o_lo(dve, t)
                    if h == 5 and t.attend:
                        find_zero(t, 0)
                    if h == 7 and t.before().finish:
                        normalise(t.before())
                    if h in (8, 9) and t.project:
                        save_v(t, h - 8)
                    if h == 8 and t.attend:
                        read_flag(t, 0)
                    if h == 9 and t.attend:
                        mask(t, 0)
                    if h == (11 if t.c == B - 1 else 10) and t.finish:
                        residual(t, 0)
                if t.attend:
                    find_zero(t, 1)

            steps(dve, step)


_INS = ["x", "xT", "adj", "wqT", "wkT", "wvT", "bv", "woT", "bo"]


def kernel(x, adj, L0_gnn_Wq, L0_gnn_Wk, L0_gnn_Wv, L0_gnn_bv, L0_gnn_Wo, L0_gnn_bo):
    import numpy as np
    import concourse.bacc as bacc
    from concourse.bass_utils import run_bass_kernel_spmd

    def grouped(w):
        return np.asarray(w).reshape(JH, KC, HD, D).transpose(3, 1, 2, 0).reshape(D, D)

    arrays = {
        "x": np.asarray(x), "xT": np.asarray(x).transpose(0, 2, 1), "adj": np.asarray(adj),
        "wqT": grouped(L0_gnn_Wq), "wkT": grouped(L0_gnn_Wk), "wvT": np.asarray(L0_gnn_Wv).T,
        "bv": np.asarray(L0_gnn_bv), "woT": np.asarray(L0_gnn_Wo).T, "bo": np.asarray(L0_gnn_bo),
    }
    arrays = {k: np.ascontiguousarray(a) for k, a in arrays.items()}
    nc = bacc.Bacc("TRN2", target_bir_lowering=False, num_devices=1)
    args = [nc.dram_tensor(f"in_{k}", arrays[k].shape, mybir.dt.from_np(arrays[k].dtype), kind="ExternalInput").ap()
            for k in _INS]
    y = nc.dram_tensor("out_y", (B, N, D), F32, kind="ExternalOutput").ap()
    build(nc, *args, y)
    r = run_bass_kernel_spmd(nc, [{f"in_{k}": arrays[k] for k in _INS}], core_ids=[0])
    return r.results[0]["out_y"]
```
